# Optimizing a Trainium2 kernel written in Bass

```python
import numpy as np
import jax
import jax.numpy as jnp

def _softmax(x, axis=-1):
    return jax.nn.softmax(x, axis=axis)

def _gelu(x):
    return jax.nn.gelu(x, approximate=True)

def _silu(x):
    return jax.nn.silu(x)

def _sigmoid(x):
    return jax.nn.sigmoid(x)

def _layernorm(x, axis=-1, eps=1e-05):
    m = jnp.mean(x, axis=axis, keepdims=True)
    v = jnp.var(x, axis=axis, keepdims=True)
    return (x - m) / jnp.sqrt(v + eps)

def _scatter_add(tgt, idx, src, axis=0):
    return tgt.at[idx].add(src)

def _segment_sum(src, seg, n):
    return jax.ops.segment_sum(src, seg, n)
kernel_name = 'mk_gnn_resnorm_d2_gnn_r32_b120cd'

def setup_inputs(seed: int=0):
    np.random.seed(seed)
    _w = jnp.asarray

    def _rec_inputs():
        import jax
        import jax.numpy as jnp
        _gk = jax.random.key(seed)
        x = -0.0005121 + 1.001 * jax.random.normal(jax.random.fold_in(_gk, 1), (3125, 160), jnp.float32)
        src = jax.random.randint(jax.random.fold_in(_gk, 2), (100000,), 0, 3125, jnp.int32)
        dst = jnp.minimum((3125 * jax.random.uniform(jax.random.fold_in(_gk, 3), (100000,)) ** 2.0).astype(jnp.int32), 99999)
        _o = jnp.argsort(dst, stable=True)
        src = src[_o]
        dst = dst[_o]
        edge_attr_16 = -0.000191324 + 0.999809 * jax.random.normal(jax.random.fold_in(_gk, 12), (100000, 16), jnp.float32)
        edge_attr_4 = 0.000126197 + 0.999763 * jax.random.normal(jax.random.fold_in(_gk, 13), (100000, 4), jnp.float32)
        edge_attr_8 = jax.random.uniform(jax.random.fold_in(_gk, 14), (100000, 8), jnp.float32, 0.0, 1)
        node_vec1 = jax.random.uniform(jax.random.fold_in(_gk, 15), (3125, 1), jnp.float32, 0.0, 1)
        return (x, src, dst, edge_attr_16, edge_attr_4, edge_attr_8, node_vec1)
    x, src, dst, edge_attr_16, edge_attr_4, edge_attr_8, node_vec1 = _rec_inputs()

    def _L0_gnn_setup():
        import jax, jax.numpy as jnp
        import numpy as np
        N = 625
        E = 10000
        MUL0 = 64
        MUL1 = 32
        FC_IN = 16
        FC_H = 64
        WNUM = 192
        key = jax.random.key(seed)
        ks = jax.random.split(key, 16)
        return {'x': jax.random.normal(ks[0], (N, MUL0 + 3 * MUL1), jnp.float32), 'node_attr': jnp.ones((N, 1), jnp.float32), 'edge_scalars': jax.random.normal(ks[1], (E, FC_IN), jnp.float32), 'edge_attr_sh': jax.random.normal(ks[2], (E, 4), jnp.float32), 'edge_src': jax.random.randint(ks[3], (E,), 0, N), 'edge_dst': jax.random.randint(ks[4], (E,), 0, N), 'Wfc1': jax.random.normal(ks[5], (FC_IN, FC_H), jnp.float32), 'Wfc2': jax.random.normal(ks[6], (FC_H, WNUM), jnp.float32), 'Wsc0': jax.random.normal(ks[7], (MUL0, MUL0), jnp.float32), 'Wsc1': jax.random.normal(ks[8], (MUL1, MUL1), jnp.float32), 'Wl1_0': jax.random.normal(ks[9], (MUL0, MUL0), jnp.float32), 'Wl1_1': jax.random.normal(ks[10], (MUL1, MUL1), jnp.float32), 'Wl2_s': jax.random.normal(ks[11], (MUL0 + MUL1, MUL0), jnp.float32), 'Wl2_v': jax.random.normal(ks[12], (MUL0 + MUL1, MUL1), jnp.float32), 'Wa': 0.1 * jax.random.normal(ks[13], (MUL0 + MUL1, 1), jnp.float32)}
    _L0_gnn_all = _L0_gnn_setup()
    _L0_gnn_in = {k: v for k, v in _L0_gnn_all.items() if k in ('Wfc1', 'Wfc2', 'Wsc0', 'Wsc1', 'Wl1_0', 'Wl1_1', 'Wl2_s', 'Wl2_v', 'Wa')}
    del _L0_gnn_all

    def _L1_gnn_setup():
        import jax, jax.numpy as jnp
        import numpy as np
        N = 1250
        E = 12500
        MUL0, MUL1 = (64, 32)
        RAD, HID = (8, 64)
        WNUM = 192
        NUM_NEIGHBORS = 10.0
        INV3 = 1.0 / np.sqrt(3.0)

        def _lin(s, v, Ws, Wv, attr):
            out_s = s @ Ws * attr * (1.0 / np.sqrt(Ws.shape[0]))
            out_v = jnp.einsum('nud,uv->nvd', v, Wv) * attr[..., None] * (1.0 / np.sqrt(Wv.shape[0]))
            return (out_s, out_v)
        key = jax.random.key(seed)
        ks = jax.random.split(key, 16)
        return {'node_input': jax.random.normal(ks[0], (N, MUL0 + 3 * MUL1), jnp.float32), 'node_attr': jnp.ones((N, 1), jnp.float32), 'edge_attr': jax.random.normal(ks[1], (E, 4), jnp.float32), 'edge_scalars': jax.random.uniform(ks[2], (E, RAD), jnp.float32), 'W_sc_s': jax.random.normal(ks[3], (MUL0, MUL0), jnp.float32), 'W_sc_v': jax.random.normal(ks[4], (MUL1, MUL1), jnp.float32), 'W1_s': jax.random.normal(ks[5], (MUL0, MUL0), jnp.float32), 'W1_v': jax.random.normal(ks[6], (MUL1, MUL1), jnp.float32), 'W2_s': jax.random.normal(ks[7], (MUL0 + MUL1, MUL0), jnp.float32), 'W2_v': jax.random.normal(ks[8], (MUL0 + MUL1, MUL1), jnp.float32), 'W3': jax.random.normal(ks[9], (MUL0 + MUL1, 1), jnp.float32), 'fcW1': jax.random.normal(ks[10], (RAD, HID), jnp.float32), 'fcW2': jax.random.normal(ks[11], (HID, WNUM), jnp.float32), 'edge_src': jax.random.randint(ks[12], (E,), 0, N, jnp.int32), 'edge_dst': jax.random.randint(ks[13], (E,), 0, N, jnp.int32)}
    _L1_gnn_all = _L1_gnn_setup()
    _L1_gnn_in = {k: v for k, v in _L1_gnn_all.items() if k in ('W_sc_s', 'W_sc_v', 'W1_s', 'W1_v', 'W2_s', 'W2_v', 'W3', 'fcW1', 'fcW2')}
    del _L1_gnn_all
    return {'x': x, 'src': src, 'dst': dst, 'edge_attr_16': edge_attr_16, 'edge_attr_4': edge_attr_4, 'edge_attr_8': edge_attr_8, 'node_vec1': node_vec1, 'L0_gnn_Wfc1': _L0_gnn_in['Wfc1'], 'L0_gnn_Wfc2': _L0_gnn_in['Wfc2'], 'L0_gnn_Wsc0': _L0_gnn_in['Wsc0'], 'L0_gnn_Wsc1': _L0_gnn_in['Wsc1'], 'L0_gnn_Wl1_0': _L0_gnn_in['Wl1_0'], 'L0_gnn_Wl1_1': _L0_gnn_in['Wl1_1'], 'L0_gnn_Wl2_s': _L0_gnn_in['Wl2_s'], 'L0_gnn_Wl2_v': _L0_gnn_in['Wl2_v'], 'L0_gnn_Wa': _L0_gnn_in['Wa'], 'L1_gnn_W_sc_s': _L1_gnn_in['W_sc_s'], 'L1_gnn_W_sc_v': _L1_gnn_in['W_sc_v'], 'L1_gnn_W1_s': _L1_gnn_in['W1_s'], 'L1_gnn_W1_v': _L1_gnn_in['W1_v'], 'L1_gnn_W2_s': _L1_gnn_in['W2_s'], 'L1_gnn_W2_v': _L1_gnn_in['W2_v'], 'L1_gnn_W3': _L1_gnn_in['W3'], 'L1_gnn_fcW1': _L1_gnn_in['fcW1'], 'L1_gnn_fcW2': _L1_gnn_in['fcW2']}

def reference(x, src, dst, edge_attr_16, edge_attr_4, edge_attr_8, node_vec1, L0_gnn_Wfc1, L0_gnn_Wfc2, L0_gnn_Wsc0, L0_gnn_Wsc1, L0_gnn_Wl1_0, L0_gnn_Wl1_1, L0_gnn_Wl2_s, L0_gnn_Wl2_v, L0_gnn_Wa, L1_gnn_W_sc_s, L1_gnn_W_sc_v, L1_gnn_W1_s, L1_gnn_W1_v, L1_gnn_W2_s, L1_gnn_W2_v, L1_gnn_W3, L1_gnn_fcW1, L1_gnn_fcW2):
    import jax
    import jax.numpy as jnp

    def _L0_gnn_ref(x, node_attr, edge_scalars, edge_attr_sh, edge_src, edge_dst, Wfc1, Wfc2, Wsc0, Wsc1, Wl1_0, Wl1_1, Wl2_s, Wl2_v, Wa):
        import jax, jax.numpy as jnp
        import numpy as np
        N = 625
        E = 10000
        MUL0 = 64
        MUL1 = 32
        FC_IN = 16
        FC_H = 64
        WNUM = 192
        n = x.shape[0]
        x0 = x[:, :MUL0]
        x1 = x[:, MUL0:].reshape(n, MUL1, 3)
        a = node_attr
        h = jax.nn.silu(edge_scalars @ (Wfc1 / jnp.sqrt(jnp.float32(FC_IN))))
        w = h @ (Wfc2 / jnp.sqrt(jnp.float32(FC_H)))
        w0 = w[:, :64]
        w1 = w[:, 64:128]
        w2 = w[:, 128:160]
        w3 = w[:, 160:192]
        inv8 = 1.0 / jnp.sqrt(jnp.float32(MUL0))
        inv32 = 1.0 / jnp.sqrt(jnp.float32(MUL1))
        sc = jnp.concatenate([x0 @ Wsc0 * a * inv8, (jnp.einsum('num,uv->nvm', x1, Wsc1) * a[..., None] * inv32).reshape(n, 3 * MUL1)], axis=1)
        f0 = x0 @ Wl1_0 * a * inv8
        f1 = jnp.einsum('num,uv->nvm', x1, Wl1_1) * a[..., None] * inv32
        e0 = f0[edge_src]
        e1 = f1[edge_src]
        sh0 = edge_attr_sh[:, :1]
        sh1 = edge_attr_sh[:, 1:4]
        mid0 = w0 * e0 * sh0
        mid1 = w3 * jnp.einsum('eum,em->eu', e1, sh1) / jnp.sqrt(3.0)
        mid2 = w1[:, :, None] * e0[:, :, None] * sh1[:, None, :]
        mid3 = w2[:, :, None] * e1 * sh0[:, :, None]
        cnt = jnp.clip(jax.ops.segment_sum(jnp.ones(edge_dst.shape, x.dtype), edge_dst, num_segments=n), 1.0)

        def smean(v):
            s = jax.ops.segment_sum(v, edge_dst, num_segments=n)
            return s / cnt.reshape((n,) + (1,) * (v.ndim - 1))
        n0, n1 = (smean(mid0), smean(mid1))
        n2, n3 = (smean(mid2), smean(mid3))
        scal = jnp.concatenate([n0, n1], axis=1)
        vec = jnp.concatenate([n2, n3], axis=1)
        inv96 = 1.0 / jnp.sqrt(jnp.float32(MUL0 + MUL1))
        alpha = scal @ Wa * a * inv96
        out_s = scal @ Wl2_s * a * inv96
        out_v = jnp.einsum('num,uv->nvm', vec, Wl2_v) * a[..., None] * inv96
        conv = jnp.concatenate([out_s, out_v.reshape(n, 3 * MUL1)], axis=1)
        return sc + alpha * conv

    def _L1_gnn_ref(node_input, node_attr, edge_attr, edge_scalars, W_sc_s, W_sc_v, W1_s, W1_v, W2_s, W2_v, W3, fcW1, fcW2, edge_src, edge_dst):
        import jax, jax.numpy as jnp
        import numpy as np
        N = 1250
        E = 12500
        MUL0, MUL1 = (64, 32)
        RAD, HID = (8, 64)
        WNUM = 192
        NUM_NEIGHBORS = 10.0
        INV3 = 1.0 / np.sqrt(3.0)

        def _lin(s, v, Ws, Wv, attr):
            out_s = s @ Ws * attr * (1.0 / np.sqrt(Ws.shape[0]))
            out_v = jnp.einsum('nud,uv->nvd', v, Wv) * attr[..., None] * (1.0 / np.sqrt(Wv.shape[0]))
            return (out_s, out_v)
        n = node_input.shape[0]
        s_in = node_input[:, :MUL0]
        v_in = node_input[:, MUL0:].reshape(n, MUL1, 3)
        sc_s, sc_v = _lin(s_in, v_in, W_sc_s, W_sc_v, node_attr)
        f_s, f_v = _lin(s_in, v_in, W1_s, W1_v, node_attr)
        h = jax.nn.silu(edge_scalars @ fcW1 * (1.0 / np.sqrt(RAD)))
        w = h @ fcW2 * (1.0 / np.sqrt(HID))
        wA, wB, wC, wD = (w[:, :64], w[:, 64:128], w[:, 128:160], w[:, 160:192])
        xs = f_s[edge_src]
        xv = f_v[edge_src]
        y0 = edge_attr[:, :1]
        y1 = edge_attr[:, 1:4]
        outA = wA * xs * y0
        outD = wD * jnp.einsum('eud,ed->eu', xv, y1) * INV3
        outB = wB[:, :, None] * xs[:, :, None] * y1[:, None, :]
        outC = wC[:, :, None] * xv * y0[:, :, None]
        edge_feat = jnp.concatenate([outA, outD, outB.reshape(-1, MUL0 * 3), outC.reshape(-1, MUL1 * 3)], axis=1)
        agg = jax.ops.segment_sum(edge_feat, edge_dst, num_segments=n)
        agg = agg * (1.0 / np.sqrt(NUM_NEIGHBORS))
        ms = agg[:, :MUL0 + MUL1]
        mv = agg[:, MUL0 + MUL1:].reshape(n, MUL0 + MUL1, 3)
        c_s, c_v = _lin(ms, mv, W2_s, W2_v, node_attr)
        conv = jnp.concatenate([c_s, c_v.reshape(n, -1)], axis=1)
        sc = jnp.concatenate([sc_s, sc_v.reshape(n, -1)], axis=1)
        angle = 0.1 * (ms @ W3) * node_attr * (1.0 / np.sqrt(MUL0 + MUL1))
        cos, sin = (jnp.cos(angle), jnp.sin(angle))
        return cos * sc + sin * conv
    x = _layernorm(x + _L0_gnn_ref(x, node_vec1, edge_attr_16, edge_attr_4, src, dst, L0_gnn_Wfc1, L0_gnn_Wfc2, L0_gnn_Wsc0, L0_gnn_Wsc1, L0_gnn_Wl1_0, L0_gnn_Wl1_1, L0_gnn_Wl2_s, L0_gnn_Wl2_v, L0_gnn_Wa), axis=-1)
    x = _layernorm(x + _L1_gnn_ref(x, node_vec1, edge_attr_4, edge_attr_8, L1_gnn_W_sc_s, L1_gnn_W_sc_v, L1_gnn_W1_s, L1_gnn_W1_v, L1_gnn_W2_s, L1_gnn_W2_v, L1_gnn_W3, L1_gnn_fcW1, L1_gnn_fcW2, src, dst), axis=-1)
    return x

_drawn_inputs = setup_inputs


def setup_inputs(seed=0):
    import zlib

    import numpy as np

    out = dict(_drawn_inputs(seed))
    spreads = {}
    factors = {'edge_attr_16': 8.0,
     'edge_attr_4': 7.11,
     'edge_attr_8': 8.0,
     'L0_gnn_Wfc1': 8.0,
     'L0_gnn_Wfc2': 8.0,
     'L0_gnn_Wl1_0': 8.0,
     'L0_gnn_Wl1_1': 8.0,
     'L0_gnn_Wl2_s': 8.0,
     'L0_gnn_Wl2_v': 8.0,
     'L0_gnn_Wa': 8.0,
     'L1_gnn_W1_s': 5.987,
     'L1_gnn_W1_v': 8.0,
     'L1_gnn_W2_s': 8.0,
     'L1_gnn_W2_v': 8.0,
     'L1_gnn_W3': 7.853,
     'L1_gnn_fcW1': 7.397,
     'L1_gnn_fcW2': 7.094}
    for name, (base, spread) in spreads.items():
        noise = np.random.default_rng([zlib.crc32(name.encode()), seed]).standard_normal(out[name].shape)
        drawn = base * np.exp(spread * noise) if base else spread * noise
        out[name] = jnp.asarray(drawn.astype(out[name].dtype))
    for name, factor in factors.items():
        out[name] = (out[name] * factor).astype(out[name].dtype)
    return out
```

```python
import math
from contextlib import ExitStack

import concourse.bass as bass
from concourse import mybir

N, D = 3125, 160
E = 100000
S0, V1 = 64, 32
VF = 3 * V1
NT = 25
NP = N // NT
P = 128
U = 4
SE = U * P
NS = -(-E // SE)
NB = NS // 4
WIN = 97
WX = 64
WX_SHIFT = 6
CH = VF + 1
NPAD = 3232
GT = 5
NG = NT // GT
HC = SE // 2
WCOL = 256

C_FC1 = 0
C_FC2 = C_FC1 + 128
C_A = C_FC2 + 192
C_B = C_A + 128
C_S = C_B + 192
C_V = C_S + 66
C_END = C_V + 32

PI_HI = 3.140625
PI_MID = math.floor((math.pi - PI_HI) * 2 ** 20) / 2 ** 20
PI_LO = math.pi - PI_HI - PI_MID
ROUND = 1.5 * 2 ** 23
FC_SCALE = (1.0 / math.sqrt(16), 1.0 / math.sqrt(8))
NODE0, NODE1 = 16, 29


def gnn(nc, x_nodes, x_t, src_t, sh_t, es0_t, es1_t, dst_t, dst_rows, attr, wts0, wts1, ftab, out):
    fp32, i32 = mybir.dt.float32, mybir.dt.int32
    ALU, ACT, AX = mybir.AluOpType, mybir.ActivationFunctionType, mybir.AxisListType
    ds = bass.ds
    es_t = [es0_t, es1_t]
    ctx = ExitStack()
    with ctx:
        def sb(name, shape, dt=fp32):
            return ctx.enter_context(nc.sbuf_tensor(name, shape, dt))

        def sem(name):
            return ctx.enter_context(nc.semaphore(name))

        wts = [sb(f"w_sb{l}", [P, C_END]) for l in range(2)]
        ident = sb("ident", [P, P])
        iota_i = sb("iota_i", [P, WIN], i32)
        iota = sb("iota", [P, WIN])
        ones_row = sb("ones_row", [1, P])
        a_sb = sb("a_sb", [NP, NT])
        a2 = sb("a2", [NP, NT])
        a_ang = sb("a_ang", [NP, NT])
        a_conv = sb("a_conv", [NP, NT])
        dst_i = sb("dst_i", [P, NS * U], i32)
        rel = sb("rel", [P, 2, NS * U])
        rows_i = sb("rows_i", [NS // 2, 2, SE], i32)
        lo_hi = sb("lo_hi", [NS // 2, 2, 2], i32)
        more = sb("more", [NS // 2, 2, 2], i32)
        base_i = sb("base_i", [1, NS], i32)
        more_i = sb("more_i", [1, NS], i32)
        base_f = sb("base_f", [1, NS])
        more_f = sb("more_f", [1, NS])
        zero_f = sb("zero_f", [1, NS])
        extra_at = sb("extra_at", [1, NS + 4], i32)
        body_row = sb("body_row", [1, 8 * (NB + 1)], i32)
        X = sb("X", [NP, NT, D])
        Y = sb("Y", [NP, NT, D])
        F = sb("F", [NP, NT, D])
        Z = sb("Z", [NP, NT, 2 + D])
        acc = sb("acc", [CH, 4, NPAD])
        xT = sb("xT", [VF, 2, GT, NP])
        stage = sb("stage", [CH, GT, 4, NP])
        v_g = sb("v_g", [NP, GT, D])
        sq_g = sb("sq_g", [NP, GT, D])
        xn_g = sb("xn_g", [NP, GT, D])
        small = sb("small", [NP, 16, GT])
        mark = sb("mark", [1, 1])
        idx = sb("idx", [P, 2, 2 * U], i32)
        sh = sb("sh", [P, 2, 2 * U, 4])
        es = sb("es", [P, HC])
        e_src = sb("e_src", [P, 4, U, D])
        e_sh0 = sb("e_sh0", [P, 2, U, D])
        sig = sb("sig", [P, 2, HC])
        hT = sb("hT", [P, 2, HC])
        em = sb("em", [P, U, 3, V1])
        t1 = sb("t1", [P, U, V1])
        t2 = sb("t2", [P, 2, U, V1])
        p1 = sb("p1", [P, 2, U, S0])
        msg = sb("msg", [P, 2, U, 4, CH])
        hot = sb("hot", [P, 2, U, WIN])
        hot_x = sb("hot_x", [P, U, WX])
        PS = ctx.enter_context(nc.psum_tensor("PS", [P, 8, 512], fp32))

        def h_ps(k):
            return PS[:, k, 0:HC]

        def w_ps(k):
            return PS[:, 2 + 2 * k:4 + 2 * k, :].rearrange("p b (j c) -> p (b j) c", c=WCOL)

        def s_ps(k):
            return PS[0:CH, 6 + k, 0:4 * WIN].rearrange("p (c w) -> p c w", w=WIN)

        s_const = sem("s_const")
        s_wts = sem("s_wts")
        s_attr = sem("s_attr")
        s_xld = sem("s_xld")
        s_dst = sem("s_dst")
        s_rows = sem("s_rows")
        s_lohi = sem("s_lohi")
        s_tab = sem("s_tab")
        s_setup = sem("s_setup")
        s_wready = sem("s_wready")
        s_agg = sem("s_agg")
        s_basef = sem("s_basef")
        s_bb = sem("s_bb")
        s_xtab = sem("s_xtab")
        s_acc0 = sem("s_acc0")
        s_xT = sem("s_xT")
        s_pre = sem("s_pre")
        s_f = sem("s_f")
        s_ftab = sem("s_ftab")
        s_tr = sem("s_tr")
        s_trc = sem("s_trc")
        s_idx = [sem(f"s_idx{k}") for k in range(2)]
        s_sh = [sem(f"s_sh{k}") for k in range(2)]
        s_es = [sem(f"s_es{k}") for k in range(2)]
        s_gath = [sem(f"s_gath{k}") for k in range(4)]
        s_go = sem("s_go")
        s_h = sem("s_h")
        s_sig = sem("s_sig")
        s_hT = sem("s_hT")
        s_w = sem("s_w")
        s_esh = sem("s_esh")
        s_em = sem("s_em")
        s_t1 = sem("s_t1")
        s_t2 = sem("s_t2")
        s_p1 = sem("s_p1")
        s_wfree = sem("s_wfree")
        s_msg = sem("s_msg")
        s_n2 = sem("s_n2")
        s_scat = sem("s_scat")
        s_acc = sem("s_acc")
        s_xrel = [sem(f"s_xrel{l}") for l in range(2)]
        s_xhot = [sem(f"s_xhot{l}") for l in range(2)]
        s_xscat = [sem(f"s_xscat{l}") for l in range(2)]
        s_xadd = [sem(f"s_xadd{l}") for l in range(2)]
        s_stage = sem("s_stage")
        s_conv = sem("s_conv")
        s_z = sem("s_z")
        s_node = sem("s_node")
        s_sin = sem("s_sin")
        s_sq = sem("s_sq")
        s_cen = sem("s_cen")
        s_sqrt = sem("s_sqrt")
        s_xn = sem("s_xn")
        s_xcopy = sem("s_xcopy")
        s_out = sem("s_out")

        block = ctx.enter_context(nc.Block())
        out_v = out.rearrange("(p i) f -> p (i f)", i=NT)
        ftab_v = ftab.rearrange("(p i) f -> p (i f)", i=NT)
        x_v = x_nodes.rearrange("(p i) f -> p i f", i=NT)
        xs_v = x_t[0:S0, :].rearrange("f (g n) -> f g n", g=NG)
        xv_v = x_t[S0:D, :].rearrange("f (g n) -> f g n", g=NG)

        @block.sync
        def _(sp):
            sp.dma_start(rows_i[:, :, :], dst_rows).then_inc(s_rows, 16)
            sp.dma_start(dst_i[:, :], dst_t).then_inc(s_dst, 16)
            sp.dma_start(xT[0:S0, 0, :, :].rearrange("f k n -> f (k n)"), xs_v[:, 0, :]).then_inc(s_xT, 16)
            sp.dma_start(xT[0:VF, 1, :, :].rearrange("f k n -> f (k n)"), xv_v[:, 0, :]).then_inc(s_xT, 16)
            sp.dma_start(wts[0][:, :], wts0).then_inc(s_wts, 16)
            sp.dma_start(wts[1][:, :], wts1).then_inc(s_wts, 16)
            sp.dma_start(a_sb[:, :], attr.rearrange("(p i) o -> p (i o)", i=NT)).then_inc(s_attr, 16)
            sp.dma_start(X[:, :, :], x_v).then_inc(s_xld, 16)
            sp.wait_ge(s_lohi, 1)
            sp.dma_start(base_i[0:1, :], more[:, 0, :]).then_inc(s_tab, 16)
            sp.dma_start(more_i[0:1, :], more[:, 1, :]).then_inc(s_tab, 16)

            def load_half(l, b, half, first):
                B = NB * l + b
                if not first:
                    sp.wait_ge(s_gath[2 * half], 64 * B)
                    sp.wait_ge(s_gath[2 * half + 1], 64 * B)
                sp.dma_start(idx[:, half, :], src_t[:, ds((b * 2 + half) * 2 * U, 2 * U)]).then_inc(s_idx[half], 16)
                if not first:
                    sp.wait_ge(s_tab, 32)
                    sp.wait_ge(s_msg, 4 * B + 2 * half - 2)
                    sp.wait_ge(s_n2, 4 * B + 2 * half - 2)
                sp.dma_start(sh[:, half, :, :].rearrange("p k c -> p (k c)"),
                             sh_t[:, ds((b * 2 + half) * 2 * U * 4, 2 * U * 4)]).then_inc(s_sh[half], 16)

            def load_es(l, b, half, first):
                B = NB * l + b
                if not first:
                    sp.wait_ge(s_h, 4 * B + 2 * half - 2)
                sp.dma_start(es[64 * half:64 * half + 64, :], es_t[l][ds((b * 2 + half) * 64, 64), :]).then_inc(s_es[half], 16)

            def layer_loads(l):
                for half in range(2):
                    load_es(l, 0, half, l == 0)
                    load_half(l, 0, half, l == 0)
                with sp.Fori(1, NB) as b:
                    for half in range(2):
                        load_es(l, b, half, False)
                        load_half(l, b, half, False)

            def table_out(l):
                with sp.Fori(0, NG) as g:
                    sp.wait_ge(s_f, NT * l + GT * (g + 1))
                    sp.dma_start(ftab_v[:, ds(GT * D * g, GT * D)],
                                 F[:, ds(GT * g, GT), :].rearrange("p i f -> p (i f)")).then_inc(s_ftab, 16)

            with sp.Fori(1, NG) as g:
                sp.wait_ge(s_pre, GT * g)
                sp.dma_start(xT[0:S0, 0, :, :].rearrange("f k n -> f (k n)"), xs_v[:, ds(g, 1), :].rearrange("f a n -> f (a n)")).then_inc(s_xT, 16)
                sp.dma_start(xT[0:VF, 1, :, :].rearrange("f k n -> f (k n)"), xv_v[:, ds(g, 1), :].rearrange("f a n -> f (a n)")).then_inc(s_xT, 16)
            table_out(0)
            layer_loads(0)
            table_out(1)
            layer_loads(1)
            with sp.Fori(0, NG) as g:
                sp.wait_ge(s_xcopy, NG + g + 1)
                sp.dma_start(out_v[:, ds(GT * D * g, GT * D)],
                             X[:, ds(GT * g, GT), :].rearrange("p i f -> p (i f)")).then_inc(s_out, 16)
            sp.wait_ge(s_out, 16 * NG)

        @block.gpsimd
        def _(pool):
            pool.memset(ident[:, :], 0.0).then_inc(s_const, 1)
            pool.iota(iota_i[:, :], pattern=[[1, WIN]], base=0, channel_multiplier=0).then_inc(s_const, 1)
            pool.memset(msg[:, :, :, :, VF:CH], 1.0).then_inc(s_const, 1)
            pool.memset(ones_row[:, :], 1.0).then_inc(s_const, 1)
            pool.wait_ge(s_const, 4)
            pool.affine_select(out=ident[:, :], in_=ident[:, :], compare_op=ALU.not_equal, fill=1.0,
                               base=0, pattern=[[-1, P]], channel_multiplier=1).then_inc(s_const, 1)
            pool.memset(acc[:, :, :], 0.0).then_inc(s_acc0, 1)

            def gather_body(l, b, first):
                B = NB * l + b
                for q in range(4):
                    half = q // 2
                    pool.wait_ge(s_ftab, 16 * NG * (l + 1))
                    if q % 2 == 0:
                        pool.wait_ge(s_idx[half], 16 * (B + 1))
                    if not first:
                        pool.wait_ge(s_msg, 4 * B + q - 3)
                        pool.wait_ge(s_esh, 4 * B + q - 3)
                    pool.sem_inc(s_go, 1)
                    for u in range(U):
                        k = (q % 2) * U + u
                        pool.indirect_dma_start(out=e_src[:, q, u, :], out_offset=None, in_=ftab,
                                                in_offset=bass.IndirectOffsetOnAxis(ap=idx[:, half, k:k + 1], axis=0)
                                                ).then_inc(s_gath[q], 16)

            def keep_rows(l, g):
                pool.wait_ge(s_xn, NG * l + g + 1)
                pool.tensor_copy(X[:, ds(GT * g, GT), :], xn_g[:, :, :]).then_inc(s_xcopy, 1)

            for l in range(2):
                gather_body(l, 0, l == 0)
                with pool.Fori(1, NB) as b:
                    gather_body(l, b, False)
                keep_rows(l, 0)
                with pool.Fori(1, NG) as g:
                    keep_rows(l, g)
                if l == 0:
                    pool.wait_ge(s_stage, NT)
                    pool.memset(acc[:, :, :], 0.0).then_inc(s_acc0, 1)

        @block.scalar
        def _(act):
            def gate(l, T, k):
                act.wait_ge(s_h, T + 1)
                if not (isinstance(T, int) and T < 2):
                    act.wait_ge(s_hT, T - 1)
                act.activation(sig[:, k, :], h_ps(k), ACT.Sigmoid, scale=FC_SCALE[l]).then_inc(s_sig, 1)

            def edge_body(l, b, last):
                B = NB * l + b
                for q in range(4):
                    T = 4 * B + q
                    half, k = q // 2, q % 2
                    if not (last and q == 3):
                        gate(l, T + 1, 1 - k)
                    act.wait_ge(s_gath[q], 64 * (B + 1))
                    if k == 0:
                        act.wait_ge(s_sh[half], 16 * (B + 1))
                    if not (isinstance(T, int) and T < 2):
                        act.wait_ge(s_wfree, T - 1)
                    for u in range(U):
                        ins = act.activation(e_sh0[:, k, u, :], e_src[:, q, u, :], ACT.Copy,
                                             scale=sh[:, half, k * U + u, 0:1])
                    ins.then_inc(s_esh, 1)
                    act.wait_ge(s_p1, T + 1)
                    for u in range(U):
                        for m in range(1, 3):
                            ins = act.activation(msg[:, k, u, 1 + m, 0:S0], p1[:, k, u, :], ACT.Copy,
                                                 scale=sh[:, half, k * U + u, 1 + m:2 + m])
                    ins.then_inc(s_n2, 1)

            def table_out_of_psum(l, g):
                for k in range(GT):
                    i = GT * g + k
                    act.wait_ge(s_pre, NT * l + i + 1)
                    bank = PS[0:NP, 4 + k % 2, :]
                    act.activation(F[:, ds(i, 1), :].rearrange("p a f -> p (a f)"), bank[:, 0:D], ACT.Copy,
                                   scale=a_sb[:, ds(i, 1)])
                    act.activation(Y[:, ds(i, 1), :].rearrange("p a f -> p (a f)"), bank[:, D:2 * D], ACT.Copy,
                                   scale=a_sb[:, ds(i, 1)]).then_inc(s_f, 1)

            def aggregate_out(l, g):
                by_tile = acc[:, :, 0:N].rearrange("q c (p i) -> q c i p", i=NT)
                for k in range(GT):
                    act.activation(stage[:, k, :, :],
                                   by_tile[:, :, ds(GT * g + k, 1), :].rearrange("q c a p -> q c (a p)"),
                                   ACT.Copy).then_inc(s_stage, 1)
                for k in range(GT):
                    i = GT * g + k
                    act.wait_ge(s_conv, NT * l + i + 1)
                    act.activation(Z[:, ds(i, 1), :].rearrange("p a f -> p (a f)"),
                                   PS[0:NP, k % 2, 0:2 + D], ACT.Copy).then_inc(s_z, 1)

            def node_group(l, g):
                aggregate_out(l, g)
                if l == 1:
                    act.wait_ge(s_node, NODE0 * NG + NODE1 * g + 7)
                    act.activation(small[:, 8, :], small[:, 4, :], ACT.Sin)
                    act.activation(small[:, 9, :], small[:, 4, :], ACT.Sin, scale=0.5).then_inc(s_sin, 1)
                act.wait_ge(s_cen, NG * l + g + 1)
                act.activation(sq_g[:, :, :], v_g[:, :, :], ACT.Square).then_inc(s_sq, 1)
                act.wait_ge(s_node, NODE0 * NG * l + (NODE0, NODE1)[l] * (g + 1) - 5)
                act.activation(small[:, 13, :], small[:, 12, :], ACT.Sqrt).then_inc(s_sqrt, 1)
                if l == 0:
                    for k in range(GT):
                        act.wait_ge(s_tr, GT * g + k + 1)
                        act.activation(xT[0:S0, 0, k, :], PS[0:S0, 2 + k % 2, 0:NP], ACT.Copy)
                        act.activation(xT[0:VF, 1, k, :], PS[0:VF, 2 + k % 2, 128:128 + NP],
                                       ACT.Copy).then_inc(s_trc, 1)
                    table_out_of_psum(1, g)

            act.wait_ge(s_attr, 16)
            table_out_of_psum(0, 0)
            with act.Fori(1, NG) as g:
                table_out_of_psum(0, g)
            for l in range(2):
                gate(l, NS * l, 0)
                edge_body(l, 0, False)
                with act.Fori(1, NB - 1) as b:
                    edge_body(l, b, False)
                edge_body(l, NB - 1, True)
                act.wait_ge(s_agg, l + 1)
                node_group(l, 0)
                with act.Fori(1, NG) as g:
                    node_group(l, g)

        @block.vector
        def _(vec):
            done = [0]

            def then(ins):
                done[0] += 1
                ins.then_inc(s_setup, 1)
                vec.wait_ge(s_setup, done[0])

            vec.wait_ge(s_rows, 16)
            vec.tensor_reduce(more[:, 0, :], rows_i[:, :, :], AX.X, ALU.min)
            then(vec.tensor_reduce(lo_hi[:, 1, :], rows_i[:, :, :], AX.X, ALU.max))
            then(vec.tensor_tensor(lo_hi[:, 0, :], lo_hi[:, 1, :], more[:, 0, :], ALU.subtract))
            then(vec.tensor_scalar(lo_hi[:, 1, :], lo_hi[:, 0, :], WX - WIN, 0, ALU.add, ALU.max))
            vec.tensor_scalar(more[:, 1, :], lo_hi[:, 1, :], WX_SHIFT, None, ALU.arith_shift_right).then_inc(s_lohi, 1)
            vec.wait_ge(s_wts, 32)
            for l in range(2):
                for sl, c in ((wts[l][0:S0, C_A:C_A + S0], 1.0 / 64), (wts[l][0:S0, C_A + S0:C_A + 2 * S0], 1.0 / 8),
                              (wts[l][0:VF, C_B:C_B + VF], 1.0 / (8 * math.sqrt(32))),
                              (wts[l][0:VF, C_B + VF:C_B + 2 * VF], 1.0 / math.sqrt(32)),
                              (wts[l][S0:VF, C_S:C_S + 66], 1.0 / math.sqrt(3))):
                    vec.tensor_scalar(sl, sl, c, None, ALU.mult).then_inc(s_wready, 1)
            vec.wait_ge(s_attr, 16)
            vec.tensor_scalar(a_ang[:, :], a_sb[:, :], 0.1 / math.sqrt(960), None, ALU.mult)
            vec.tensor_scalar(a_conv[:, :], a_sb[:, :], 1.0 / math.sqrt(960), None, ALU.mult)
            then(vec.tensor_tensor(a2[:, :], a_sb[:, :], a_sb[:, :], ALU.mult))
            then(vec.tensor_scalar(a2[:, :], a2[:, :], 1.0 / 96, None, ALU.mult))
            vec.memset(extra_at[:, :], 0)
            vec.memset(body_row[:, :], 0)
            vec.memset(zero_f[:, :], 0.0)
            vec.wait_ge(s_const, 5)
            then(vec.tensor_copy(iota[:, :], iota_i[:, :]))
            vec.wait_ge(s_tab, 32)
            vec.tensor_copy(base_f[:, :], base_i[:, :]).then_inc(s_basef, 1)
            then(vec.tensor_copy(more_f[:, :], more_i[:, :]))
            vec.tensor_tensor_scan(extra_at[0:1, 1:NS + 1], more_f[:, :], zero_f[:, :], 0.0, ALU.add,
                                   ALU.add).then_inc(s_xtab, 1)
            rows = body_row[0:1, :].rearrange("p (b c) -> p b c", c=8)
            by_body = base_i[0:1, :].rearrange("p (b q) -> p b q", q=4)
            extra_by_body = extra_at[0:1, 0:NS].rearrange("p (b q) -> p b q", q=4)
            vec.tensor_copy(rows[:, 0:NB, 1:4], by_body[:, :, 0:3])
            vec.tensor_copy(rows[:, 1:NB + 1, 0:1], by_body[:, :, 3:4])
            vec.wait_ge(s_xtab, 1)
            vec.tensor_copy(rows[:, 0:NB, 5:6], extra_by_body[:, :, 3:4])
            vec.tensor_copy(rows[:, 0:NB, 6:7], extra_by_body[:, :, 0:1])
            vec.tensor_copy(rows[:, 1:NB + 1, 4:5], extra_by_body[:, :, 3:4])
            vec.tensor_copy(rows[:, 0:NB, 7:8], extra_at[0:1, 4:NS + 4].rearrange("p (b q) -> p b q", q=4)[:, :, 0:1])\
                .then_inc(s_xtab, 1)
            vec.wait_ge(s_bb, 1)
            vec.wait_ge(s_dst, 16)
            for l in range(2):
                ins = vec.tensor_tensor(rel[:, l, :].rearrange("p (s u) -> p s u", u=U),
                                        dst_i[:, :].rearrange("p (s u) -> p s u", u=U),
                                        PS[:, 7, 0:NS].unsqueeze(2).broadcast_to([P, NS, U]), ALU.subtract)
            then(ins)
            vec.wait_ge(s_xtab, 2)

            def add_window(k, at, width):
                part = acc[:, :, ds(at, width)]
                return vec.tensor_tensor(part, part, s_ps(k)[:, :, 0:width], ALU.add)

            def is_hot(out_hot, l, s, first, width):
                return vec.tensor_tensor(out_hot, rel[:, l, ds(U * s, U)].unsqueeze(2).broadcast_to([P, U, width]),
                                         iota[:, first:first + width].unsqueeze(1).broadcast_to([P, U, width]),
                                         ALU.is_equal)

            row_regs = [vec.alloc_register(f"v_row{j}") for j in range(6)]

            def row_of(b):
                vec.load(row_regs, body_row[0:1, ds(8 * b, 6)])
                return ([vec.snap(r, min_val=0, max_val=N - 1) for r in row_regs[0:4]]
                        + [vec.snap(r, min_val=0, max_val=NS * 49) for r in row_regs[4:6]])

            def extra_before(s):
                return vec.value_load(extra_at[0:1, ds(s, 1)], min_val=0, max_val=NS * 49)

            def add_up(l, s, k, base):
                T = NS * l + s
                vec.wait_ge(s_scat, T + 1)
                if not (isinstance(T, int) and T == 0):
                    vec.wait_ge(s_acc, T)
                add_window(k, base, WIN).then_inc(s_acc, 1)

            def add_further(l, s, k, base):
                T = NS * l + s
                v0, v1 = extra_before(s), extra_before(s + 1)
                with vec.If(v1 > v0):
                    with vec.Fori(v0, v1) as v:
                        vec.wait_ge(s_acc, T + 1)
                        part = rel[:, l, ds(U * s, U)]
                        vec.tensor_scalar(part, part, float(WX), None, ALU.subtract).then_inc(s_xrel[l], 1)
                        vec.wait_ge(s_xrel[l], v + 1)
                        is_hot(hot_x[:, :, :], l, s, WIN - WX, WX).then_inc(s_xhot[l], 1)
                        vec.wait_ge(s_xscat[l], v + 1)
                        at = nc.s_assert_within(base + WX * (v - v0) + WIN, 0, NPAD - WX,
                                                skip_runtime_bounds_check_because="it is at most the largest dst")
                        add_window(k, at, WX).then_inc(s_xadd[l], 1)
                        vec.wait_ge(s_xadd[l], v + 1)

            def sh_of(q):
                return sh[:, q // 2, (q % 2) * U:(q % 2) * U + U, :]

            def hidden(l, T, k):
                vec.wait_ge(s_sig, T + 1)
                vec.scalar_tensor_tensor(out=hT[:, k, :], in0=h_ps(k), scalar=FC_SCALE[l], in1=sig[:, k, :],
                                         op0=ALU.mult, op1=ALU.mult).then_inc(s_hT, 1)

            def vector_rows(T, q, B):
                vec.wait_ge(s_gath[q], 64 * (B + 1))
                if q % 2 == 0:
                    vec.wait_ge(s_sh[q // 2], 16 * (B + 1))
                vec.tensor_tensor(em[:, :, :, :], e_src[:, q, :, S0:D].rearrange("p u (m v) -> p u m v", v=V1),
                                  sh_of(q)[:, :, 1:4].unsqueeze(3).broadcast_to([P, U, 3, V1]),
                                  ALU.mult).then_inc(s_em, 1)

            def rows_summed(l, s, T, k):
                vec.wait_ge(s_em, T + 1)
                vec.tensor_tensor(t1[:, :, :], em[:, :, 0, :], em[:, :, 1, :], ALU.add).then_inc(s_t1, 1)
                is_hot(hot[:, k, :, :], l, s, 0, WIN)
                vec.wait_ge(s_t1, T + 1)
                vec.tensor_tensor(t2[:, k, :, :], t1[:, :, :], em[:, :, 2, :], ALU.add).then_inc(s_t2, 1)

            def edge_body(l, b, first, last):
                *base, before, after = row_of(b)
                with vec.If(after > before):
                    edge_steps(l, b, first, last, base, True)
                with vec.Else():
                    edge_steps(l, b, first, last, base, False)

            def edge_steps(l, b, first, last, base, further):
                B = NB * l + b
                for q in range(4):
                    s, T = 4 * b + q, 4 * B + q
                    k = q % 2
                    w = w_ps(k)
                    out_m = msg[:, k, :, :, :]
                    if not (last and q == 3):
                        hidden(l, T + 1, 1 - k)
                    vec.wait_ge(s_w, T + 1)
                    vec.tensor_tensor(p1[:, k, :, :], w[:, :, 64:128], e_src[:, q, :, 0:S0], ALU.mult).then_inc(s_p1, 1)
                    vec.wait_ge(s_esh, T + 1)
                    vec.tensor_tensor(out_m[:, :, 0, 0:S0], w[:, :, 0:64], e_sh0[:, k, :, 0:S0], ALU.mult)
                    vec.tensor_tensor(out_m[:, :, 1:4, S0:VF],
                                      w[:, :, 128:160].unsqueeze(2).broadcast_to([P, U, 3, V1]),
                                      e_sh0[:, k, :, S0:D].rearrange("p u (m v) -> p u m v", v=V1), ALU.mult)
                    vec.wait_ge(s_t2, T + 1)
                    vec.tensor_tensor(out_m[:, :, 0, S0:VF], w[:, :, 160:192], t2[:, k, :, :],
                                      ALU.mult).then_inc(s_wfree, 1)
                    vec.wait_ge(s_p1, T + 1)
                    vec.tensor_tensor(out_m[:, :, 1, 0:S0], p1[:, k, :, :],
                                      sh_of(q)[:, :, 1:2].broadcast_to([P, U, S0]), ALU.mult).then_inc(s_msg, 1)
                    if not (last and q == 3):
                        vector_rows(T + 1, (q + 1) % 4, B + (q + 1) // 4)
                    if not (first and q == 0):
                        add_up(l, s - 1, 1 - k, base[q])
                    if not (last and q == 3):
                        rows_summed(l, s + 1, T + 1, 1 - k)
                    if further and not (first and q == 0):
                        add_further(l, s - 1, 1 - k, base[q])

            def node_group(l, g):
                first_step = NODE0 * NG * l + (NODE0, NODE1)[l] * g
                step = [0]

                def then(ins):
                    step[0] += 1
                    ins.then_inc(s_node, 1)
                    vec.wait_ge(s_node, first_step + step[0])

                def sm(j):
                    return small[:, j, :]

                def wide(ap):
                    return ap.unsqueeze(2).broadcast_to([NP, GT, D])

                z = Z[:, ds(GT * g, GT), :]
                alpha = z[:, :, 1:2].rearrange("p i a -> p (i a)")
                conv = z[:, :, 2:2 + D]
                self_con = Y[:, ds(GT * g, GT), :]
                v = v_g[:, :, :]
                vec.wait_ge(s_z, NT * l + GT * (g + 1))
                if l == 0:
                    count = z[:, :, 0:1].rearrange("p i a -> p (i a)")
                    then(vec.tensor_scalar(sm(0), count, 1.0, None, ALU.max))
                    then(vec.reciprocal(sm(1), sm(0)))
                    then(vec.tensor_tensor(sm(2), alpha, sm(1), ALU.mult))
                    then(vec.tensor_tensor(sm(3), sm(1), a2[:, ds(GT * g, GT)], ALU.mult))
                    then(vec.tensor_tensor(sm(4), sm(2), sm(3), ALU.mult))
                    then(vec.tensor_tensor(v, conv, wide(sm(4)), ALU.mult))
                    then(vec.tensor_tensor(v, v, self_con, ALU.add))
                else:
                    then(vec.tensor_tensor(sm(0), alpha, a_ang[:, ds(GT * g, GT)], ALU.mult))
                    then(vec.tensor_scalar(sm(1), sm(0), 1.0 / math.pi, ROUND, ALU.mult, ALU.add))
                    then(vec.tensor_scalar(sm(2), sm(1), ROUND, None, ALU.subtract))
                    then(vec.scalar_tensor_tensor(out=sm(3), in0=sm(2), scalar=-PI_HI, in1=sm(0),
                                                  op0=ALU.mult, op1=ALU.add))
                    then(vec.scalar_tensor_tensor(out=sm(3), in0=sm(2), scalar=-PI_MID, in1=sm(3),
                                                  op0=ALU.mult, op1=ALU.add))
                    then(vec.scalar_tensor_tensor(out=sm(3), in0=sm(2), scalar=-PI_LO, in1=sm(3),
                                                  op0=ALU.mult, op1=ALU.add))
                    then(vec.tensor_scalar(sm(4), sm(3), -3.1415925, 3.1415925, ALU.max, ALU.min))
                    assert step[0] == 7
                    then(vec.tensor_scalar(sm(5), sm(2), 0.5, ROUND, ALU.mult, ALU.add))
                    then(vec.tensor_scalar(sm(6), sm(5), ROUND, None, ALU.subtract))
                    then(vec.scalar_tensor_tensor(out=sm(5), in0=sm(6), scalar=-2.0, in1=sm(2),
                                                  op0=ALU.mult, op1=ALU.add))
                    then(vec.tensor_tensor(sm(6), sm(5), sm(5), ALU.mult))
                    then(vec.tensor_scalar(sm(7), sm(6), -2.0, 1.0, ALU.mult, ALU.add))
                    vec.wait_ge(s_sin, g + 1)
                    then(vec.tensor_tensor(sm(5), sm(9), sm(9), ALU.mult))
                    then(vec.tensor_scalar(sm(5), sm(5), -2.0, 1.0, ALU.mult, ALU.add))
                    then(vec.tensor_tensor(sm(6), sm(5), sm(7), ALU.mult))
                    then(vec.tensor_tensor(sm(1), sm(8), sm(7), ALU.mult))
                    then(vec.tensor_tensor(sm(7), sm(1), a_conv[:, ds(GT * g, GT)], ALU.mult))
                    then(vec.tensor_tensor(v, conv, wide(sm(7)), ALU.mult))
                    then(vec.tensor_tensor(sq_g[:, :, :], self_con, wide(sm(6)), ALU.mult))
                    then(vec.tensor_tensor(v, v, sq_g[:, :, :], ALU.add))
                vec.wait_ge(s_xld, 16)
                then(vec.tensor_tensor(v, v, X[:, ds(GT * g, GT), :], ALU.add))
                then(vec.tensor_reduce(sm(10), v, AX.X, ALU.add))
                vec.scalar_tensor_tensor(out=v, in0=wide(sm(10)), scalar=-1.0 / D, in1=v,
                                         op0=ALU.mult, op1=ALU.add).then_inc(s_cen, 1)
                vec.wait_ge(s_sq, NG * l + g + 1)
                then(vec.tensor_reduce(sm(11), sq_g[:, :, :], AX.X, ALU.add))
                then(vec.tensor_scalar(sm(12), sm(11), 1.0 / D, 1e-5, ALU.mult, ALU.add))
                vec.wait_ge(s_sqrt, NG * l + g + 1)
                then(vec.reciprocal(sm(14), sm(13)))
                then(vec.tensor_tensor(sm(10), sm(14), sm(14), ALU.mult))
                then(vec.tensor_tensor(sm(11), sm(10), sm(12), ALU.mult))
                then(vec.tensor_scalar(sm(10), sm(11), -0.5, 1.5, ALU.mult, ALU.add))
                then(vec.tensor_tensor(sm(15), sm(14), sm(10), ALU.mult))
                vec.wait_ge(s_xcopy, NG * l + g)
                if l == 0:
                    vec.wait_ge(s_tr, GT * g)
                vec.tensor_tensor(xn_g[:, :, :], v, wide(sm(15)), ALU.mult).then_inc(s_xn, 1)
                assert step[0] == (NODE0, NODE1)[l]

            for l in range(2):
                vec.wait_ge(s_acc0, l + 1)
                T = NS * l
                hidden(l, T, 0)
                vector_rows(T, 0, NB * l)
                rows_summed(l, 0, T, 0)
                edge_body(l, 0, True, False)
                with vec.Fori(1, NB - 1) as b:
                    edge_body(l, b, False, False)
                edge_body(l, NB - 1, False, True)
                base = row_of(NB)[0]
                add_up(l, NS - 1, 1, base)
                add_further(l, NS - 1, 1, base)
                vec.wait_ge(s_acc, NS * (l + 1))
                vec.memset(mark[:, :], 0.0).then_inc(s_agg, 1)
                node_group(l, 0)
                with vec.Fori(1, NG) as g:
                    node_group(l, g)

        @block.tensor
        def _(pe):
            def hidden(l, T, q, B):
                if q % 2 == 0:
                    pe.wait_ge(s_es[q // 2], 16 * (B + 1))
                if not (isinstance(T, int) and T < 2):
                    pe.wait_ge(s_hT, T - 1)
                r = slice(32 * q, 32 * q + 32)
                pe.matmul(h_ps(q % 2), wts[l][r, C_FC1:C_FC1 + P], es[r, :], start=True, stop=True).then_inc(s_h, 1)

            def edge_weights(l, T, k):
                pe.wait_ge(s_hT, T + 1)
                if not (isinstance(T, int) and T < 2):
                    pe.wait_ge(s_wfree, T - 1)
                for u in range(U):
                    r = slice(64 * (u // 2), 64 * (u // 2) + 64)
                    ins = pe.matmul(w_ps(k)[:, u, 0:192], hT[r, k, (u % 2) * P:(u % 2) * P + P],
                                    wts[l][r, C_FC2:C_FC2 + 192], start=True, stop=True)
                ins.then_inc(s_w, 1)

            def sums(k, onehot, width):
                for c in range(4):
                    for u in range(U):
                        ins = pe.matmul(s_ps(k)[:, c, 0:width], msg[:, k, u, c, :], onehot[:, u, :],
                                        start=(u == 0), stop=(u == U - 1))
                return ins

            row_regs = [pe.alloc_register(f"t_row{j}") for j in range(2)]

            def extra_before(s):
                return pe.value_load(extra_at[0:1, ds(s, 1)], min_val=0, max_val=NS * 49)

            def edge_body(l, b, last):
                pe.load(row_regs, body_row[0:1, ds(8 * b + 6, 2)])
                before, after = [pe.snap(r, min_val=0, max_val=NS * 49) for r in row_regs]
                with pe.If(after > before):
                    edge_steps(l, b, last, True)
                with pe.Else():
                    edge_steps(l, b, last, False)

            def edge_steps(l, b, last, further):
                B = NB * l + b
                for q in range(4):
                    s, T = 4 * b + q, 4 * B + q
                    k = q % 2
                    if not (last and q >= 2):
                        hidden(l, T + 2, (q + 2) % 4, B + (q + 2) // 4)
                    if not (last and q == 3):
                        edge_weights(l, T + 1, 1 - k)
                    pe.wait_ge(s_msg, T + 1)
                    pe.wait_ge(s_n2, T + 1)
                    if not (isinstance(T, int) and T < 2):
                        pe.wait_ge(s_acc, T - 1)
                    sums(k, hot[:, k, :, :], WIN).then_inc(s_scat, 1)
                    if further:
                        v0, v1 = extra_before(s), extra_before(s + 1)
                        with pe.If(v1 > v0):
                            with pe.Fori(v0, v1) as v:
                                pe.wait_ge(s_xhot[l], v + 1)
                                sums(k, hot_x[:, :, :], WX).then_inc(s_xscat[l], 1)

            def node_products(l, g):
                for k in range(GT):
                    i = GT * g + k
                    if l == 0:
                        if k == 0:
                            pe.wait_ge(s_xT, 32 * (g + 1))
                    else:
                        pe.wait_ge(s_trc, i + 1)
                    pe.wait_ge(s_f, NT * l + (i if k == 0 else i - 1))
                    bank = PS[0:NP, 4 + k % 2, :]
                    xs, xv = xT[0:S0, 0, k, :], xT[0:VF, 1, k, :]
                    W = wts[l]
                    pe.matmul(bank[:, 0:S0], xs, W[0:S0, C_A:C_A + S0], start=True, stop=True)
                    pe.matmul(bank[:, S0:D], xv, W[0:VF, C_B:C_B + VF], start=True, stop=True)
                    pe.matmul(bank[:, D:D + S0], xs, W[0:S0, C_A + S0:C_A + 2 * S0], start=True, stop=True)
                    pe.matmul(bank[:, D + S0:2 * D], xv, W[0:VF, C_B + VF:C_B + 2 * VF],
                              start=True, stop=True).then_inc(s_pre, 1)

            def conv_products(l, g):
                W = wts[l]
                for k in range(GT):
                    i = GT * g + k
                    pe.wait_ge(s_stage, NT * l + i + 1)
                    pe.wait_ge(s_z, NT * l + (i if k == 0 else i - 1))
                    bank = PS[0:NP, k % 2, :]
                    st = stage[:, k, :, :]
                    pe.matmul(bank[:, 0:66], st[:, 0, :], W[0:CH, C_S:C_S + 66], start=True, stop=True)
                    for m in range(3):
                        o = 66 + V1 * m
                        ins = pe.matmul(bank[:, o:o + V1], st[0:VF, 1 + m, :], W[0:VF, C_V:C_V + V1],
                                        start=True, stop=True)
                    ins.then_inc(s_conv, 1)

            def node_group(l, g):
                conv_products(l, g)
                if l == 0:
                    pe.wait_ge(s_xn, g + 1)
                    for k in range(GT):
                        pe.wait_ge(s_trc, GT * g + (k if k == 0 else k - 1))
                        pe.sem_inc(s_go, 1)
                        bank = PS[:, 2 + k % 2, :]
                        pe.transpose(bank[0:S0, 0:NP], xn_g[:, k, 0:S0], ident[0:NP, 0:NP])
                        pe.transpose(bank[0:VF, 128:128 + NP], xn_g[:, k, S0:D],
                                     ident[0:NP, 0:NP]).then_inc(s_tr, 1)
                    node_products(1, g)

            pe.wait_ge(s_const, 5)
            pe.wait_ge(s_wready, 10)
            node_products(0, 0)
            with pe.Fori(1, NG) as g:
                node_products(0, g)
            pe.wait_ge(s_basef, 1)
            pe.matmul(PS[:, 7, 0:NS], ones_row[:, :], base_f[:, :], start=True, stop=True).then_inc(s_bb, 1)
            pe.wait_ge(s_xtab, 2)
            for l in range(2):
                pe.wait_ge(s_f, NT * (l + 1))
                if l == 1:
                    pe.wait_ge(s_z, NT)
                hidden(l, NS * l, 0, NB * l)
                hidden(l, NS * l + 1, 1, NB * l)
                edge_weights(l, NS * l, 0)
                edge_body(l, 0, False)
                with pe.Fori(1, NB - 1) as b:
                    edge_body(l, b, False)
                edge_body(l, NB - 1, True)
                node_group(l, 0)
                with pe.Fori(1, NG) as g:
                    node_group(l, g)


def kernel(x, src, dst, edge_attr_16, edge_attr_4, edge_attr_8, node_vec1, **w):
    import numpy as np
    import concourse.bacc as bacc
    from concourse.bass_utils import run_bass_kernel_spmd

    x, src, dst = np.asarray(x), np.asarray(src), np.asarray(dst)
    x_m = np.concatenate([x[:, :S0], x[:, S0:].reshape(N, V1, 3).transpose(0, 2, 1).reshape(N, VF)], axis=1)
    x_t = x_m.reshape(NP, NT, D).transpose(2, 1, 0).reshape(D, N)
    pad = NS * SE - E

    def by_tile(a):
        return a.reshape(NS * U, P, -1).transpose(1, 0, 2).reshape(P, -1)

    src_t = by_tile(np.pad(src, (0, pad)))
    sh_t = by_tile(np.pad(np.asarray(edge_attr_4), ((0, pad), (0, 0))))
    dst_t = by_tile(np.pad(dst, (0, pad), constant_values=-1))
    dst_rows = np.pad(dst, (0, pad), mode="edge").reshape(NS // 2, 2, SE)

    def radial(a):
        a = np.pad(np.asarray(a), ((0, pad), (0, 16 - a.shape[1])))
        return a.reshape(NS, 2, HC, 16).transpose(0, 1, 3, 2).reshape(NS * 32, HC)

    def weights(fc1, fc2, s_f, s_self, v_f, v_self, alpha, l2s, l2v):
        t = np.zeros((P, C_END), np.float32)
        for k in range(8):
            r = 16 * k
            t[r:r + fc1.shape[0], C_FC1 + 64 * (k % 2):C_FC1 + 64 * (k % 2) + 64] = fc1
        for k in range(2):
            t[64 * k:64 * k + 64, C_FC2:C_FC2 + 192] = fc2
        t[0:S0, C_A:C_A + S0] = s_f
        t[0:S0, C_A + S0:C_A + 2 * S0] = s_self
        for m in range(3):
            r, c = slice(V1 * m, V1 * m + V1), C_B + V1 * m
            t[r, c:c + V1] = v_f
            t[r, c + VF:c + VF + V1] = v_self
        t[VF, C_S] = 1.0
        t[0:VF, C_S + 1:C_S + 2] = alpha
        t[0:VF, C_S + 2:C_S + 66] = l2s
        t[0:VF, C_V:C_V + V1] = l2v
        return t

    w = {k: np.asarray(v) for k, v in w.items()}
    wts0 = weights(w["L0_gnn_Wfc1"], w["L0_gnn_Wfc2"], w["L0_gnn_Wl1_0"], w["L0_gnn_Wsc0"], w["L0_gnn_Wl1_1"],
                   w["L0_gnn_Wsc1"], w["L0_gnn_Wa"], w["L0_gnn_Wl2_s"], w["L0_gnn_Wl2_v"])
    wts1 = weights(w["L1_gnn_fcW1"], w["L1_gnn_fcW2"], w["L1_gnn_W1_s"], w["L1_gnn_W_sc_s"], w["L1_gnn_W1_v"],
                   w["L1_gnn_W_sc_v"], w["L1_gnn_W3"], w["L1_gnn_W2_s"], w["L1_gnn_W2_v"])

    nc = bacc.Bacc("TRN2", target_bir_lowering=False, num_devices=1)
    arrays, args = {}, []
    for name, a in (("x_nodes", x_m), ("x_t", x_t), ("src_t", src_t), ("sh_t", sh_t), ("es0_t", radial(edge_attr_16)),
                    ("es1_t", radial(edge_attr_8)), ("dst_t", dst_t), ("dst_rows", dst_rows),
                    ("attr", np.asarray(node_vec1)), ("wts0", wts0), ("wts1", wts1)):
        a = np.ascontiguousarray(a)
        arrays[name] = a
        args.append(nc.dram_tensor(name, a.shape, mybir.dt.from_np(a.dtype), kind="ExternalInput").ap())
    args.append(nc.dram_tensor("ftab", (N, D), mybir.dt.float32, kind="Internal").ap())
    args.append(nc.dram_tensor("nodes_out", (N, D), mybir.dt.float32, kind="ExternalOutput").ap())
    gnn(nc, *args)
    r = run_bass_kernel_spmd(nc, [arrays], core_ids=[0])
    y = r.results[0]["nodes_out"]
    return np.concatenate([y[:, :S0], y[:, S0:].reshape(N, 3, V1).transpose(0, 2, 1).reshape(N, VF)], axis=1)
```

```python
import math
from contextlib import ExitStack

import concourse.bass as bass
from concourse import mybir

N, D = 3125, 160
E = 100000
S0, V1 = 64, 32
VF = 3 * V1
NT = 25
NP = N // NT
P = 128
U = 4
SE = U * P
NS = -(-E // SE)
NB = NS // 4
WIN = 97
WX = 64
WX_SHIFT = 6
CH = VF + 1
NPAD = 3232
GT = 5
NG = NT // GT
HC = SE // 2
WCOL = 256

C_FC1 = 0
C_FC2 = C_FC1 + 128
C_A = C_FC2 + 192
C_B = C_A + 128
C_S = C_B + 192
C_V = C_S + 66
C_END = C_V + 32

PI_HI = 3.140625
PI_MID = math.floor((math.pi - PI_HI) * 2 ** 20) / 2 ** 20
PI_LO = math.pi - PI_HI - PI_MID
ROUND = 1.5 * 2 ** 23
FC_SCALE = (1.0 / math.sqrt(16), 1.0 / math.sqrt(8))
NODE0, NODE1 = 16, 29
ZC = 2 + D
BANKS = ((0, 3), (3, 2))
TR_BANK = (2, 6)
PROD_BANK = (4, 5, 2, 3, 6)


def gnn(nc, x_nodes, x_t, src_t, sh_t, es0_t, es1_t, dst_t, dst_rows, attr, wts0, wts1, ftab, out):
    fp32, i32 = mybir.dt.float32, mybir.dt.int32
    ALU, ACT, AX = mybir.AluOpType, mybir.ActivationFunctionType, mybir.AxisListType
    ds = bass.ds
    es_t = [es0_t, es1_t]
    ctx = ExitStack()
    with ctx:
        def sb(name, shape, dt=fp32):
            return ctx.enter_context(nc.sbuf_tensor(name, shape, dt))

        def sem(name):
            return ctx.enter_context(nc.semaphore(name))

        wts = [sb(f"w_sb{l}", [P, C_END]) for l in range(2)]
        ident = sb("ident", [P, P])
        iota_i = sb("iota_i", [P, WIN], i32)
        iota = sb("iota", [P, WIN])
        ones_row = sb("ones_row", [1, P])
        a_sb = sb("a_sb", [NP, NT])
        a2 = sb("a2", [NP, NT])
        a_ang = sb("a_ang", [NP, NT])
        a_conv = sb("a_conv", [NP, NT])
        dst_i = sb("dst_i", [P, NS * U], i32)
        rel = sb("rel", [P, 2, NS * U])
        rows_i = sb("rows_i", [NS // 2, 2, SE], i32)
        lo_hi = sb("lo_hi", [NS // 2, 2, 2], i32)
        more = sb("more", [NS // 2, 2, 2], i32)
        base_i = sb("base_i", [1, NS], i32)
        more_i = sb("more_i", [1, NS], i32)
        base_f = sb("base_f", [1, NS])
        more_f = sb("more_f", [1, NS])
        zero_f = sb("zero_f", [1, NS])
        extra_at = sb("extra_at", [1, NS + 4], i32)
        body_row = sb("body_row", [1, 8 * (NB + 1)], i32)
        X = sb("X", [NP, NT, D])
        FY = sb("FY", [NP, 2, NT, D])
        Z = sb("Z", [NP, NT, 2 + D])
        acc = sb("acc", [CH, 4, NPAD])
        xT = sb("xT", [VF, GT, 2, NP])
        stage = sb("stage", [CH, GT, 4, NP])
        v_g = sb("v_g", [NP, GT, D])
        sq_g = sb("sq_g", [NP, GT, D])
        xn_g = sb("xn_g", [NP, GT, D])
        small = sb("small", [NP, 16, GT])
        idx = sb("idx", [P, 2, 2 * U], i32)
        sh = sb("sh", [P, 2, 2 * U, 4])
        es = sb("es", [P, HC])
        e_src = sb("e_src", [P, 4, U, D])
        e_sh0 = sb("e_sh0", [P, 2, U, D])
        sig = sb("sig", [P, 2, HC])
        hT = sb("hT", [P, 2, HC])
        em = sb("em", [P, U, 3, V1])
        t1 = sb("t1", [P, U, V1])
        t2 = sb("t2", [P, 2, U, V1])
        p1 = sb("p1", [P, 2, U, S0])
        msg = sb("msg", [P, 2, U, 4, CH])
        hot = sb("hot", [P, 2, U, WIN])
        hot_x = sb("hot_x", [P, U, WX])
        PS = ctx.enter_context(nc.psum_tensor("PS", [P, 8, 512], fp32))

        def h_ps(k):
            return PS[:, k, 0:HC]

        rows_01, rows_23 = [e_src[:, 2 * j:2 * j + 2, :, :].rearrange("p q u d -> p (q u d)")[:, 0:2 * GT * NP]
                            .rearrange("p (k c n) -> p k c n", k=GT, c=2) for j in range(2)]
        x_cols = [xT, stage[:, :, 0:2, :], stage[:, :, 2:4, :], rows_01, rows_23]

        def w_ps(k):
            return PS[:, 2 + 2 * k:4 + 2 * k, :].rearrange("p b (j c) -> p (b j) c", c=WCOL)

        def s_ps(k):
            return PS[0:CH, 6 + k, 0:4 * WIN].rearrange("p (c w) -> p c w", w=WIN)

        s_const = sem("s_const")
        s_wts = [sem(f"s_wts{l}") for l in range(2)]
        s_attr = sem("s_attr")
        s_xld = sem("s_xld")
        s_dst = sem("s_dst")
        s_rows = sem("s_rows")
        s_lohi = sem("s_lohi")
        s_tab = sem("s_tab")
        s_setup = sem("s_setup")
        s_wready = sem("s_wready")
        s_agg = sem("s_agg")
        s_basef = sem("s_basef")
        s_bb = sem("s_bb")
        s_xtab = sem("s_xtab")
        s_acc0 = sem("s_acc0")
        s_xT = [sem(f"s_xT{g}") for g in range(NG)]
        s_pre = sem("s_pre")
        s_f = sem("s_f")
        s_ftab = sem("s_ftab")
        s_tr = sem("s_tr")
        s_trc = sem("s_trc")
        s_idx = [sem(f"s_idx{k}") for k in range(2)]
        s_sh = [sem(f"s_sh{k}") for k in range(2)]
        s_es = [sem(f"s_es{k}") for k in range(2)]
        s_gath = [sem(f"s_gath{k}") for k in range(4)]
        s_go = sem("s_go")
        s_h = sem("s_h")
        s_sig = sem("s_sig")
        s_hT = sem("s_hT")
        s_w = sem("s_w")
        s_esh = sem("s_esh")
        s_em = sem("s_em")
        s_t1 = sem("s_t1")
        s_t2 = sem("s_t2")
        s_p1 = sem("s_p1")
        s_wfree = sem("s_wfree")
        s_msg = sem("s_msg")
        s_n2 = sem("s_n2")
        s_scat = sem("s_scat")
        s_acc = sem("s_acc")
        s_xrel = [sem(f"s_xrel{l}") for l in range(2)]
        s_xhot = [sem(f"s_xhot{l}") for l in range(2)]
        s_xscat = [sem(f"s_xscat{l}") for l in range(2)]
        s_xadd = [sem(f"s_xadd{l}") for l in range(2)]
        s_stage = sem("s_stage")
        s_conv = sem("s_conv")
        s_z = sem("s_z")
        s_node = sem("s_node")
        s_sin = sem("s_sin")
        s_sq = sem("s_sq")
        s_cen = sem("s_cen")
        s_sqrt = sem("s_sqrt")
        s_xn = sem("s_xn")
        s_xcopy = sem("s_xcopy")
        s_out = sem("s_out")

        block = ctx.enter_context(nc.Block())
        out_v = out.rearrange("(p i) f -> p (i f)", i=NT)
        ftab_v = ftab.rearrange("(p i) f -> p (i f)", i=NT)
        x_v = x_nodes.rearrange("(p i) f -> p i f", i=NT)
        xs_v = x_t[0:S0, :].rearrange("f (g n) -> f g n", g=NG)
        xv_v = x_t[S0:D, :].rearrange("f (g n) -> f g n", g=NG)

        @block.sync
        def _(sp):
            def load_x_cols(g):
                for part, view, rows in ((0, xs_v, S0), (1, xv_v, VF)):
                    sp.dma_start(x_cols[g][0:rows, :, part, :],
                                 view[:, g, :].rearrange("f (k n) -> f k n", n=NP)).then_inc(s_xT[g], 16)

            sp.dma_start(wts[0][:, :], wts0).then_inc(s_wts[0], 16)
            load_x_cols(0)
            sp.dma_start(a_sb[:, :], attr.rearrange("(p i) o -> p (i o)", i=NT)).then_inc(s_attr, 16)
            load_x_cols(1)
            sp.dma_start(rows_i[:, :, :], dst_rows).then_inc(s_rows, 16)
            load_x_cols(2)
            sp.dma_start(dst_i[:, :], dst_t).then_inc(s_dst, 16)
            load_x_cols(3)
            load_x_cols(4)
            sp.dma_start(wts[1][:, :], wts1).then_inc(s_wts[1], 16)
            sp.wait_ge(s_lohi, 1)
            sp.dma_start(base_i[0:1, :], more[:, 0, :]).then_inc(s_tab, 16)
            sp.dma_start(more_i[0:1, :], more[:, 1, :]).then_inc(s_tab, 16)

            def load_half(l, b, half, first):
                B = NB * l + b
                if not first:
                    sp.wait_ge(s_gath[2 * half], 64 * B)
                    sp.wait_ge(s_gath[2 * half + 1], 64 * B)
                sp.dma_start(idx[:, half, :], src_t[:, ds((b * 2 + half) * 2 * U, 2 * U)]).then_inc(s_idx[half], 16)
                if not first:
                    sp.wait_ge(s_tab, 32)
                    sp.wait_ge(s_msg, 4 * B + 2 * half - 2)
                    sp.wait_ge(s_n2, 4 * B + 2 * half - 2)
                sp.dma_start(sh[:, half, :, :].rearrange("p k c -> p (k c)"),
                             sh_t[:, ds((b * 2 + half) * 2 * U * 4, 2 * U * 4)]).then_inc(s_sh[half], 16)

            def load_es(l, b, half, first):
                B = NB * l + b
                if not first:
                    sp.wait_ge(s_h, 4 * B + 2 * half - 2)
                sp.dma_start(es[64 * half:64 * half + 64, :], es_t[l][ds((b * 2 + half) * 64, 64), :]).then_inc(s_es[half], 16)

            def first_loads(l):
                for half in range(2):
                    load_es(l, 0, half, l == 0)
                    load_half(l, 0, half, l == 0)

            def layer_loads(l):
                with sp.Fori(1, NB) as b:
                    for half in range(2):
                        load_es(l, b, half, False)
                        load_half(l, b, half, False)

            def table_out(l, g):
                sp.wait_ge(s_f, NT * l + GT * (g + 1))
                sp.dma_start(ftab_v[:, ds(GT * D * g, GT * D)],
                             FY[:, 0, ds(GT * g, GT), :].rearrange("p i f -> p (i f)")).then_inc(s_ftab, 16)

            first_loads(0)
            with sp.Fori(0, NG) as g:
                table_out(0, g)
            sp.dma_start(X[:, :, :], x_v).then_inc(s_xld, 16)
            layer_loads(0)
            with sp.Fori(0, NG) as g:
                table_out(1, g)
            first_loads(1)
            layer_loads(1)
            with sp.Fori(0, NG) as g:
                sp.wait_ge(s_xn, NG + g + 1)
                sp.dma_start(out_v[:, ds(GT * D * g, GT * D)],
                             X[:, ds(GT * g, GT), :].rearrange("p i f -> p (i f)")).then_inc(s_out, 16)
            sp.wait_ge(s_out, 16 * NG)

        @block.gpsimd
        def _(pool):
            pool.memset(ident[:, :], 0.0).then_inc(s_const, 1)
            pool.iota(iota_i[:, :], pattern=[[1, WIN]], base=0, channel_multiplier=0).then_inc(s_const, 1)
            pool.memset(msg[:, :, :, :, VF:CH], 1.0).then_inc(s_const, 1)
            pool.memset(ones_row[:, :], 1.0).then_inc(s_const, 1)
            pool.wait_ge(s_const, 4)
            pool.affine_select(out=ident[:, :], in_=ident[:, :], compare_op=ALU.not_equal, fill=1.0,
                               base=0, pattern=[[-1, P]], channel_multiplier=1).then_inc(s_const, 1)
            pool.memset(acc[:, :, :], 0.0).then_inc(s_acc0, 1)

            def gather_body(l, b, first):
                B = NB * l + b
                for q in range(4):
                    half = q // 2
                    pool.wait_ge(s_ftab, 16 * NG * (l + 1))
                    if q % 2 == 0:
                        pool.wait_ge(s_idx[half], 16 * (B + 1))
                    if not first:
                        pool.wait_ge(s_msg, 4 * B + q - 3)
                        pool.wait_ge(s_esh, 4 * B + q - 3)
                    pool.sem_inc(s_go, 1)
                    for u in range(U):
                        k = (q % 2) * U + u
                        pool.indirect_dma_start(out=e_src[:, q, u, :], out_offset=None, in_=ftab,
                                                in_offset=bass.IndirectOffsetOnAxis(ap=idx[:, half, k:k + 1], axis=0)
                                                ).then_inc(s_gath[q], 16)

            def keep_rows(g):
                pool.wait_ge(s_xn, g + 1)
                pool.tensor_copy(X[:, ds(GT * g, GT), :], xn_g[:, :, :]).then_inc(s_xcopy, 1)

            for l in range(2):
                gather_body(l, 0, l == 0)
                with pool.Fori(1, NB) as b:
                    gather_body(l, b, False)
                if l == 0:
                    with pool.Fori(0, NG - 1) as g:
                        keep_rows(g)
                    pool.wait_ge(s_stage, NG)
                    pool.memset(acc[:, :, :], 0.0).then_inc(s_acc0, 1)
                    keep_rows(NG - 1)

        @block.scalar
        def _(act):
            def gate(l, T, k):
                act.wait_ge(s_h, T + 1)
                if not (isinstance(T, int) and T < 2):
                    act.wait_ge(s_hT, T - 1)
                act.activation(sig[:, k, :], h_ps(k), ACT.Sigmoid, scale=FC_SCALE[l]).then_inc(s_sig, 1)

            def edge_body(l, b, last):
                B = NB * l + b
                for q in range(4):
                    T = 4 * B + q
                    half, k = q // 2, q % 2
                    if not (last and q == 3):
                        gate(l, T + 1, 1 - k)
                    act.wait_ge(s_gath[q], 64 * (B + 1))
                    if k == 0:
                        act.wait_ge(s_sh[half], 16 * (B + 1))
                    if not (isinstance(T, int) and T < 2):
                        act.wait_ge(s_wfree, T - 1)
                    for u in range(U):
                        ins = act.activation(e_sh0[:, k, u, :], e_src[:, q, u, :], ACT.Copy,
                                             scale=sh[:, half, k * U + u, 0:1])
                    ins.then_inc(s_esh, 1)
                    act.wait_ge(s_p1, T + 1)
                    for u in range(U):
                        for m in range(1, 3):
                            ins = act.activation(msg[:, k, u, 1 + m, 0:S0], p1[:, k, u, :], ACT.Copy,
                                                 scale=sh[:, half, k * U + u, 1 + m:2 + m])
                    ins.then_inc(s_n2, 1)

            def table_out_of_psum(l, g):
                for k in range(GT):
                    i = GT * g + k
                    act.wait_ge(s_pre, NT * l + i + 1)
                    bank = PS[0:NP, PROD_BANK[k], :]
                    act.activation(FY[:, :, ds(i, 1), 0:S0].rearrange("p j a f -> p j (a f)"),
                                   bank[:, 0:2 * S0].rearrange("p (j f) -> p j f", j=2), ACT.Copy, scale=a_sb[:, ds(i, 1)])
                    act.activation(FY[:, :, ds(i, 1), S0:D].rearrange("p j a f -> p j (a f)"),
                                   bank[:, 2 * S0:2 * D].rearrange("p (j f) -> p j f", j=2), ACT.Copy,
                                   scale=a_sb[:, ds(i, 1)]).then_inc(s_f, 1)

            def stage_group(l, g):
                by_tile = acc[:, :, 0:N].rearrange("q c (p i) -> q c i p", i=NT)
                act.activation(stage[:, :, :, :].rearrange("q k c p -> q c k p"), by_tile[:, :, ds(GT * g, GT), :],
                               ACT.Copy).then_inc(s_stage, 1)

            def conv_out(l, g):
                for j, (k, n) in enumerate(BANKS):
                    act.wait_ge(s_conv, 2 * (NG * l + g) + j + 1)
                    act.activation(Z[:, ds(GT * g + k, n), :],
                                   PS[0:NP, j, 0:n * ZC].rearrange("p (i f) -> p i f", f=ZC), ACT.Copy).then_inc(s_z, 1)

            def squares(l, g):
                if l == 1:
                    act.wait_ge(s_node, NODE0 * NG + NODE1 * g + 7)
                    act.activation(small[:, 8, :], small[:, 4, :], ACT.Sin)
                    act.activation(small[:, 9, :], small[:, 4, :], ACT.Sin, scale=0.5).then_inc(s_sin, 1)
                act.wait_ge(s_cen, NG * l + g + 1)
                act.activation(sq_g[:, :, :], v_g[:, :, :], ACT.Square).then_inc(s_sq, 1)

            def node_group(l, g, left):
                act.wait_ge(s_node, NODE0 * NG * l + (NODE0, NODE1)[l] * (g + 1) - 5)
                act.activation(small[:, 13, :], small[:, 12, :], ACT.Sqrt).then_inc(s_sqrt, 1)
                if left >= 1:
                    conv_out(l, g + 1)
                if left >= 2:
                    stage_group(l, g + 2)
                if l == 0:
                    for j, (k, n) in enumerate(BANKS):
                        act.wait_ge(s_tr, 2 * g + j + 1)
                        for part, rows in ((0, S0), (1, VF)):
                            ins = act.activation(xT[0:rows, k:k + n, part, :],
                                                 PS[0:rows, TR_BANK[j] + part, 0:n * NP].rearrange("f (k n) -> f k n", n=NP),
                                                 ACT.Copy)
                        ins.then_inc(s_trc, 1)
                    table_out_of_psum(1, g)
                if left >= 1:
                    squares(l, g + 1)

            act.wait_ge(s_attr, 16)
            table_out_of_psum(0, 0)
            with act.Fori(1, NG) as g:
                table_out_of_psum(0, g)
            for l in range(2):
                gate(l, NS * l, 0)
                edge_body(l, 0, False)
                with act.Fori(1, NB - 1) as b:
                    edge_body(l, b, False)
                edge_body(l, NB - 1, True)
                act.wait_ge(s_agg, l + 1)
                stage_group(l, 0)
                conv_out(l, 0)
                stage_group(l, 1)
                squares(l, 0)
                with act.Fori(0, NG - 2) as g:
                    node_group(l, g, 2)
                node_group(l, NG - 2, 1)
                node_group(l, NG - 1, 0)

        @block.vector
        def _(vec):
            done = [0]

            def then(ins):
                done[0] += 1
                ins.then_inc(s_setup, 1)
                vec.wait_ge(s_setup, done[0])

            def scale_weights(l):
                vec.wait_ge(s_wts[l], 16)
                for sl, c in ((wts[l][0:S0, C_A:C_A + S0], 1.0 / 64), (wts[l][0:S0, C_A + S0:C_A + 2 * S0], 1.0 / 8),
                              (wts[l][0:VF, C_B:C_B + VF], 1.0 / (8 * math.sqrt(32))),
                              (wts[l][0:VF, C_B + VF:C_B + 2 * VF], 1.0 / math.sqrt(32)),
                              (wts[l][S0:VF, C_S:C_S + 66], 1.0 / math.sqrt(3))):
                    vec.tensor_scalar(sl, sl, c, None, ALU.mult).then_inc(s_wready, 1)

            scale_weights(0)
            vec.wait_ge(s_rows, 16)
            vec.tensor_reduce(more[:, 0, :], rows_i[:, :, :], AX.X, ALU.min)
            then(vec.tensor_reduce(lo_hi[:, 1, :], rows_i[:, :, :], AX.X, ALU.max))
            then(vec.tensor_tensor(lo_hi[:, 0, :], lo_hi[:, 1, :], more[:, 0, :], ALU.subtract))
            then(vec.tensor_scalar(lo_hi[:, 1, :], lo_hi[:, 0, :], WX - WIN, 0, ALU.add, ALU.max))
            vec.tensor_scalar(more[:, 1, :], lo_hi[:, 1, :], WX_SHIFT, None, ALU.arith_shift_right).then_inc(s_lohi, 1)
            vec.wait_ge(s_attr, 16)
            vec.tensor_scalar(a_ang[:, :], a_sb[:, :], 0.1 / math.sqrt(960), None, ALU.mult)
            vec.tensor_scalar(a_conv[:, :], a_sb[:, :], 1.0 / math.sqrt(960), None, ALU.mult)
            then(vec.tensor_tensor(a2[:, :], a_sb[:, :], a_sb[:, :], ALU.mult))
            then(vec.tensor_scalar(a2[:, :], a2[:, :], 1.0 / 96, None, ALU.mult))
            vec.memset(extra_at[:, :], 0)
            vec.memset(body_row[:, :], 0)
            vec.memset(zero_f[:, :], 0.0)
            vec.wait_ge(s_const, 5)
            then(vec.tensor_copy(iota[:, :], iota_i[:, :]))
            vec.wait_ge(s_tab, 32)
            vec.tensor_copy(base_f[:, :], base_i[:, :]).then_inc(s_basef, 1)
            then(vec.tensor_copy(more_f[:, :], more_i[:, :]))
            vec.tensor_tensor_scan(extra_at[0:1, 1:NS + 1], more_f[:, :], zero_f[:, :], 0.0, ALU.add,
                                   ALU.add).then_inc(s_xtab, 1)
            rows = body_row[0:1, :].rearrange("p (b c) -> p b c", c=8)
            by_body = base_i[0:1, :].rearrange("p (b q) -> p b q", q=4)
            extra_by_body = extra_at[0:1, 0:NS].rearrange("p (b q) -> p b q", q=4)
            vec.tensor_copy(rows[:, 0:NB, 1:4], by_body[:, :, 0:3])
            vec.tensor_copy(rows[:, 1:NB + 1, 0:1], by_body[:, :, 3:4])
            vec.wait_ge(s_xtab, 1)
            vec.tensor_copy(rows[:, 0:NB, 5:6], extra_by_body[:, :, 3:4])
            vec.tensor_copy(rows[:, 0:NB, 6:7], extra_by_body[:, :, 0:1])
            vec.tensor_copy(rows[:, 1:NB + 1, 4:5], extra_by_body[:, :, 3:4])
            vec.tensor_copy(rows[:, 0:NB, 7:8], extra_at[0:1, 4:NS + 4].rearrange("p (b q) -> p b q", q=4)[:, :, 0:1])\
                .then_inc(s_xtab, 1)
            vec.wait_ge(s_bb, 1)
            vec.wait_ge(s_dst, 16)
            for l in range(2):
                ins = vec.tensor_tensor(rel[:, l, :].rearrange("p (s u) -> p s u", u=U),
                                        dst_i[:, :].rearrange("p (s u) -> p s u", u=U),
                                        PS[:, 7, 0:NS].unsqueeze(2).broadcast_to([P, NS, U]), ALU.subtract)
            then(ins)
            vec.wait_ge(s_xtab, 2)
            scale_weights(1)

            def add_window(k, at, width):
                part = acc[:, :, ds(at, width)]
                return vec.tensor_tensor(part, part, s_ps(k)[:, :, 0:width], ALU.add)

            def is_hot(out_hot, l, s, first, width):
                return vec.tensor_tensor(out_hot, rel[:, l, ds(U * s, U)].unsqueeze(2).broadcast_to([P, U, width]),
                                         iota[:, first:first + width].unsqueeze(1).broadcast_to([P, U, width]),
                                         ALU.is_equal)

            row_regs = [vec.alloc_register(f"v_row{j}") for j in range(6)]

            def row_of(b):
                vec.load(row_regs, body_row[0:1, ds(8 * b, 6)])
                return ([vec.snap(r, min_val=0, max_val=N - 1) for r in row_regs[0:4]]
                        + [vec.snap(r, min_val=0, max_val=NS * 49) for r in row_regs[4:6]])

            def extra_before(s):
                return vec.value_load(extra_at[0:1, ds(s, 1)], min_val=0, max_val=NS * 49)

            def add_up(l, s, k, base):
                T = NS * l + s
                vec.wait_ge(s_scat, T + 1)
                if not (isinstance(T, int) and T == 0):
                    vec.wait_ge(s_acc, T)
                add_window(k, base, WIN).then_inc(s_acc, 1)

            def add_further(l, s, k, base):
                T = NS * l + s
                v0, v1 = extra_before(s), extra_before(s + 1)
                with vec.If(v1 > v0):
                    with vec.Fori(v0, v1) as v:
                        vec.wait_ge(s_acc, T + 1)
                        part = rel[:, l, ds(U * s, U)]
                        vec.tensor_scalar(part, part, float(WX), None, ALU.subtract).then_inc(s_xrel[l], 1)
                        vec.wait_ge(s_xrel[l], v + 1)
                        is_hot(hot_x[:, :, :], l, s, WIN - WX, WX).then_inc(s_xhot[l], 1)
                        vec.wait_ge(s_xscat[l], v + 1)
                        at = nc.s_assert_within(base + WX * (v - v0) + WIN, 0, NPAD - WX,
                                                skip_runtime_bounds_check_because="it is at most the largest dst")
                        add_window(k, at, WX).then_inc(s_xadd[l], 1)
                        vec.wait_ge(s_xadd[l], v + 1)

            def sh_of(q):
                return sh[:, q // 2, (q % 2) * U:(q % 2) * U + U, :]

            def hidden(l, T, k):
                vec.wait_ge(s_sig, T + 1)
                vec.scalar_tensor_tensor(out=hT[:, k, :], in0=h_ps(k), scalar=FC_SCALE[l], in1=sig[:, k, :],
                                         op0=ALU.mult, op1=ALU.mult).then_inc(s_hT, 1)

            def vector_rows(T, q, B):
                vec.wait_ge(s_gath[q], 64 * (B + 1))
                if q % 2 == 0:
                    vec.wait_ge(s_sh[q // 2], 16 * (B + 1))
                vec.tensor_tensor(em[:, :, :, :], e_src[:, q, :, S0:D].rearrange("p u (m v) -> p u m v", v=V1),
                                  sh_of(q)[:, :, 1:4].unsqueeze(3).broadcast_to([P, U, 3, V1]),
                                  ALU.mult).then_inc(s_em, 1)

            def rows_summed(l, s, T, k):
                vec.wait_ge(s_em, T + 1)
                vec.tensor_tensor(t1[:, :, :], em[:, :, 0, :], em[:, :, 1, :], ALU.add).then_inc(s_t1, 1)
                is_hot(hot[:, k, :, :], l, s, 0, WIN)
                vec.wait_ge(s_t1, T + 1)
                vec.tensor_tensor(t2[:, k, :, :], t1[:, :, :], em[:, :, 2, :], ALU.add).then_inc(s_t2, 1)

            def edge_body(l, b, first, last):
                *base, before, after = row_of(b)
                with vec.If(after > before):
                    edge_steps(l, b, first, last, base, True)
                with vec.Else():
                    edge_steps(l, b, first, last, base, False)

            def edge_steps(l, b, first, last, base, further):
                B = NB * l + b
                for q in range(4):
                    s, T = 4 * b + q, 4 * B + q
                    k = q % 2
                    w = w_ps(k)
                    out_m = msg[:, k, :, :, :]
                    if not (last and q == 3):
                        hidden(l, T + 1, 1 - k)
                    vec.wait_ge(s_w, T + 1)
                    vec.tensor_tensor(p1[:, k, :, :], w[:, :, 64:128], e_src[:, q, :, 0:S0], ALU.mult).then_inc(s_p1, 1)
                    vec.wait_ge(s_esh, T + 1)
                    vec.tensor_tensor(out_m[:, :, 0, 0:S0], w[:, :, 0:64], e_sh0[:, k, :, 0:S0], ALU.mult)
                    vec.tensor_tensor(out_m[:, :, 1:4, S0:VF],
                                      w[:, :, 128:160].unsqueeze(2).broadcast_to([P, U, 3, V1]),
                                      e_sh0[:, k, :, S0:D].rearrange("p u (m v) -> p u m v", v=V1), ALU.mult)
                    vec.wait_ge(s_t2, T + 1)
                    vec.tensor_tensor(out_m[:, :, 0, S0:VF], w[:, :, 160:192], t2[:, k, :, :],
                                      ALU.mult).then_inc(s_wfree, 1)
                    vec.wait_ge(s_p1, T + 1)
                    vec.tensor_tensor(out_m[:, :, 1, 0:S0], p1[:, k, :, :],
                                      sh_of(q)[:, :, 1:2].broadcast_to([P, U, S0]), ALU.mult).then_inc(s_msg, 1)
                    if not (last and q == 3):
                        vector_rows(T + 1, (q + 1) % 4, B + (q + 1) // 4)
                    if not (first and q == 0):
                        add_up(l, s - 1, 1 - k, base[q])
                    if not (last and q == 3):
                        rows_summed(l, s + 1, T + 1, 1 - k)
                    if further and not (first and q == 0):
                        add_further(l, s - 1, 1 - k, base[q])

            def node_group(l, g):
                first_step = NODE0 * NG * l + (NODE0, NODE1)[l] * g
                step = [0]

                def then(ins):
                    step[0] += 1
                    ins.then_inc(s_node, 1)
                    vec.wait_ge(s_node, first_step + step[0])

                def sm(j):
                    return small[:, j, :]

                def wide(ap):
                    return ap.unsqueeze(2).broadcast_to([NP, GT, D])

                z = Z[:, ds(GT * g, GT), :]
                alpha = z[:, :, 1:2].rearrange("p i a -> p (i a)")
                conv = z[:, :, 2:2 + D]
                self_con = FY[:, 1, ds(GT * g, GT), :]
                v = v_g[:, :, :]
                vec.wait_ge(s_z, 2 * (NG * l + g + 1))
                if l == 0:
                    count = z[:, :, 0:1].rearrange("p i a -> p (i a)")
                    then(vec.tensor_scalar(sm(0), count, 1.0, None, ALU.max))
                    then(vec.reciprocal(sm(1), sm(0)))
                    then(vec.tensor_tensor(sm(2), alpha, sm(1), ALU.mult))
                    then(vec.tensor_tensor(sm(3), sm(1), a2[:, ds(GT * g, GT)], ALU.mult))
                    then(vec.tensor_tensor(sm(4), sm(2), sm(3), ALU.mult))
                    then(vec.tensor_tensor(v, conv, wide(sm(4)), ALU.mult))
                    then(vec.tensor_tensor(v, v, self_con, ALU.add))
                else:
                    then(vec.tensor_tensor(sm(0), alpha, a_ang[:, ds(GT * g, GT)], ALU.mult))
                    then(vec.tensor_scalar(sm(1), sm(0), 1.0 / math.pi, ROUND, ALU.mult, ALU.add))
                    then(vec.tensor_scalar(sm(2), sm(1), ROUND, None, ALU.subtract))
                    then(vec.scalar_tensor_tensor(out=sm(3), in0=sm(2), scalar=-PI_HI, in1=sm(0),
                                                  op0=ALU.mult, op1=ALU.add))
                    then(vec.scalar_tensor_tensor(out=sm(3), in0=sm(2), scalar=-PI_MID, in1=sm(3),
                                                  op0=ALU.mult, op1=ALU.add))
                    then(vec.scalar_tensor_tensor(out=sm(3), in0=sm(2), scalar=-PI_LO, in1=sm(3),
                                                  op0=ALU.mult, op1=ALU.add))
                    then(vec.tensor_scalar(sm(4), sm(3), -3.1415925, 3.1415925, ALU.max, ALU.min))
                    assert step[0] == 7
                    then(vec.tensor_scalar(sm(5), sm(2), 0.5, ROUND, ALU.mult, ALU.add))
                    then(vec.tensor_scalar(sm(6), sm(5), ROUND, None, ALU.subtract))
                    then(vec.scalar_tensor_tensor(out=sm(5), in0=sm(6), scalar=-2.0, in1=sm(2),
                                                  op0=ALU.mult, op1=ALU.add))
                    then(vec.tensor_tensor(sm(6), sm(5), sm(5), ALU.mult))
                    then(vec.tensor_scalar(sm(7), sm(6), -2.0, 1.0, ALU.mult, ALU.add))
                    vec.wait_ge(s_sin, g + 1)
                    then(vec.tensor_tensor(sm(5), sm(9), sm(9), ALU.mult))
                    then(vec.tensor_scalar(sm(5), sm(5), -2.0, 1.0, ALU.mult, ALU.add))
                    then(vec.tensor_tensor(sm(6), sm(5), sm(7), ALU.mult))
                    then(vec.tensor_tensor(sm(1), sm(8), sm(7), ALU.mult))
                    then(vec.tensor_tensor(sm(7), sm(1), a_conv[:, ds(GT * g, GT)], ALU.mult))
                    then(vec.tensor_tensor(v, conv, wide(sm(7)), ALU.mult))
                    then(vec.tensor_tensor(sq_g[:, :, :], self_con, wide(sm(6)), ALU.mult))
                    then(vec.tensor_tensor(v, v, sq_g[:, :, :], ALU.add))
                vec.wait_ge(s_xld, 16)
                if l == 1:
                    vec.wait_ge(s_xcopy, NG)
                then(vec.tensor_tensor(v, v, X[:, ds(GT * g, GT), :], ALU.add))
                then(vec.tensor_reduce(sm(10), v, AX.X, ALU.add))
                vec.scalar_tensor_tensor(out=v, in0=wide(sm(10)), scalar=-1.0 / D, in1=v,
                                         op0=ALU.mult, op1=ALU.add).then_inc(s_cen, 1)
                vec.wait_ge(s_sq, NG * l + g + 1)
                then(vec.tensor_reduce(sm(11), sq_g[:, :, :], AX.X, ALU.add))
                then(vec.tensor_scalar(sm(12), sm(11), 1.0 / D, 1e-5, ALU.mult, ALU.add))
                vec.wait_ge(s_sqrt, NG * l + g + 1)
                then(vec.reciprocal(sm(14), sm(13)))
                then(vec.tensor_tensor(sm(10), sm(14), sm(14), ALU.mult))
                then(vec.tensor_tensor(sm(11), sm(10), sm(12), ALU.mult))
                then(vec.tensor_scalar(sm(10), sm(11), -0.5, 1.5, ALU.mult, ALU.add))
                then(vec.tensor_tensor(sm(15), sm(14), sm(10), ALU.mult))
                if l == 0:
                    if not (isinstance(g, int) and g == 0):
                        vec.wait_ge(s_xcopy, g)
                        vec.wait_ge(s_tr, 2 * g)
                    normed = xn_g[:, :, :]
                else:
                    normed = X[:, ds(GT * g, GT), :]
                vec.tensor_tensor(normed, v, wide(sm(15)), ALU.mult).then_inc(s_xn, 1)
                assert step[0] == (NODE0, NODE1)[l]

            for l in range(2):
                vec.wait_ge(s_acc0, l + 1)
                T = NS * l
                hidden(l, T, 0)
                vector_rows(T, 0, NB * l)
                rows_summed(l, 0, T, 0)
                edge_body(l, 0, True, False)
                with vec.Fori(1, NB - 1) as b:
                    edge_body(l, b, False, False)
                edge_body(l, NB - 1, False, True)
                base = row_of(NB)[0]
                add_up(l, NS - 1, 1, base)
                add_further(l, NS - 1, 1, base)
                vec.wait_ge(s_acc, NS * (l + 1))
                vec.sem_inc(s_agg, 1)
                node_group(l, 0)
                with vec.Fori(1, NG) as g:
                    node_group(l, g)

        @block.tensor
        def _(pe):
            def hidden(l, T, q, B):
                if q % 2 == 0:
                    pe.wait_ge(s_es[q // 2], 16 * (B + 1))
                if not (isinstance(T, int) and T < 2):
                    pe.wait_ge(s_hT, T - 1)
                r = slice(32 * q, 32 * q + 32)
                pe.matmul(h_ps(q % 2), wts[l][r, C_FC1:C_FC1 + P], es[r, :], start=True, stop=True).then_inc(s_h, 1)

            def edge_weights(l, T, k):
                pe.wait_ge(s_hT, T + 1)
                if not (isinstance(T, int) and T < 2):
                    pe.wait_ge(s_wfree, T - 1)
                for u in range(U):
                    r = slice(64 * (u // 2), 64 * (u // 2) + 64)
                    ins = pe.matmul(w_ps(k)[:, u, 0:192], hT[r, k, (u % 2) * P:(u % 2) * P + P],
                                    wts[l][r, C_FC2:C_FC2 + 192], start=True, stop=True)
                ins.then_inc(s_w, 1)

            def sums(k, onehot, width):
                for c in range(4):
                    for u in range(U):
                        ins = pe.matmul(s_ps(k)[:, c, 0:width], msg[:, k, u, c, :], onehot[:, u, :],
                                        start=(u == 0), stop=(u == U - 1))
                return ins

            row_regs = [pe.alloc_register(f"t_row{j}") for j in range(2)]

            def extra_before(s):
                return pe.value_load(extra_at[0:1, ds(s, 1)], min_val=0, max_val=NS * 49)

            def edge_body(l, b, last):
                pe.load(row_regs, body_row[0:1, ds(8 * b + 6, 2)])
                before, after = [pe.snap(r, min_val=0, max_val=NS * 49) for r in row_regs]
                with pe.If(after > before):
                    edge_steps(l, b, last, True)
                with pe.Else():
                    edge_steps(l, b, last, False)

            def edge_steps(l, b, last, further):
                B = NB * l + b
                for q in range(4):
                    s, T = 4 * b + q, 4 * B + q
                    k = q % 2
                    if not (last and q >= 2):
                        hidden(l, T + 2, (q + 2) % 4, B + (q + 2) // 4)
                    if not (last and q == 3):
                        edge_weights(l, T + 1, 1 - k)
                    pe.wait_ge(s_msg, T + 1)
                    pe.wait_ge(s_n2, T + 1)
                    if not (isinstance(T, int) and T < 2):
                        pe.wait_ge(s_acc, T - 1)
                    sums(k, hot[:, k, :, :], WIN).then_inc(s_scat, 1)
                    if further:
                        v0, v1 = extra_before(s), extra_before(s + 1)
                        with pe.If(v1 > v0):
                            with pe.Fori(v0, v1) as v:
                                pe.wait_ge(s_xhot[l], v + 1)
                                sums(k, hot_x[:, :, :], WX).then_inc(s_xscat[l], 1)

            def node_products(l, g, cols):
                W = wts[l]
                for k in range(GT):
                    if l == 1:
                        pe.wait_ge(s_trc, 2 * g + (1 if k < BANKS[1][0] else 2))
                    elif g > 0:
                        pe.wait_ge(s_f, GT * (g - 1) + k + 1)
                    bank = PS[0:NP, PROD_BANK[k], :]
                    pe.matmul(bank[:, 0:2 * S0], cols[0:S0, k, 0, :], W[0:S0, C_A:C_A + 2 * S0], start=True, stop=True)
                    pe.matmul(bank[:, 2 * S0:2 * D], cols[0:VF, k, 1, :], W[0:VF, C_B:C_B + 2 * VF],
                              start=True, stop=True).then_inc(s_pre, 1)

            def conv_products(l, g):
                W = wts[l]
                pe.wait_ge(s_stage, NG * l + g + 1)
                if not (isinstance(g, int) and g == 0):
                    pe.wait_ge(s_z, 2 * (NG * l + g))
                for j, (first, n) in enumerate(BANKS):
                    for k in range(n):
                        out_k = PS[0:NP, j, ZC * k:ZC * k + ZC]
                        st = stage[:, first + k, :, :]
                        pe.matmul(out_k[:, 0:66], st[:, 0, :], W[0:CH, C_S:C_S + 66], start=True, stop=True)
                        for m in range(3):
                            o = 66 + V1 * m
                            ins = pe.matmul(out_k[:, o:o + V1], st[0:VF, 1 + m, :], W[0:VF, C_V:C_V + V1],
                                            start=True, stop=True)
                    ins.then_inc(s_conv, 1)

            def transposes(g):
                pe.wait_ge(s_xn, g + 1)
                pe.wait_ge(s_f, NT + GT * g)
                pe.sem_inc(s_go, 1)
                for j, (first, n) in enumerate(BANKS):
                    for k in range(n):
                        for part, (c0, c1) in enumerate(((0, S0), (S0, D))):
                            ins = pe.transpose(PS[0:c1 - c0, TR_BANK[j] + part, NP * k:NP * k + NP],
                                               xn_g[:, first + k, c0:c1], ident[0:NP, 0:NP])
                    ins.then_inc(s_tr, 1)

            def node_group(l, g, last):
                if not last:
                    conv_products(l, g + 1)
                if l == 0:
                    transposes(g)
                    node_products(1, g, xT)

            pe.wait_ge(s_wready, 5)
            for g in range(NG):
                pe.wait_ge(s_xT[g], 32)
                node_products(0, g, x_cols[g])
            pe.wait_ge(s_const, 5)
            pe.wait_ge(s_basef, 1)
            pe.matmul(PS[:, 7, 0:NS], ones_row[:, :], base_f[:, :], start=True, stop=True).then_inc(s_bb, 1)
            pe.wait_ge(s_xtab, 2)
            for l in range(2):
                pe.wait_ge(s_f, NT * (l + 1))
                if l == 1:
                    pe.wait_ge(s_z, 2 * NG)
                    pe.wait_ge(s_wready, 10)
                hidden(l, NS * l, 0, NB * l)
                hidden(l, NS * l + 1, 1, NB * l)
                edge_weights(l, NS * l, 0)
                edge_body(l, 0, False)
                with pe.Fori(1, NB - 1) as b:
                    edge_body(l, b, False)
                edge_body(l, NB - 1, True)
                conv_products(l, 0)
                if l == 0:
                    pe.wait_ge(s_wready, 10)
                with pe.Fori(0, NG - 1) as g:
                    node_group(l, g, False)
                node_group(l, NG - 1, True)


def kernel(x, src, dst, edge_attr_16, edge_attr_4, edge_attr_8, node_vec1, **w):
    import numpy as np
    import concourse.bacc as bacc
    from concourse.bass_utils import run_bass_kernel_spmd

    x, src, dst = np.asarray(x), np.asarray(src), np.asarray(dst)
    x_m = np.concatenate([x[:, :S0], x[:, S0:].reshape(N, V1, 3).transpose(0, 2, 1).reshape(N, VF)], axis=1)
    x_t = x_m.reshape(NP, NT, D).transpose(2, 1, 0).reshape(D, N)
    pad = NS * SE - E

    def by_tile(a):
        return a.reshape(NS * U, P, -1).transpose(1, 0, 2).reshape(P, -1)

    src_t = by_tile(np.pad(src, (0, pad)))
    sh_t = by_tile(np.pad(np.asarray(edge_attr_4), ((0, pad), (0, 0))))
    dst_t = by_tile(np.pad(dst, (0, pad), constant_values=-1))
    dst_rows = np.pad(dst, (0, pad), mode="edge").reshape(NS // 2, 2, SE)

    def radial(a):
        a = np.pad(np.asarray(a), ((0, pad), (0, 16 - a.shape[1])))
        return a.reshape(NS, 2, HC, 16).transpose(0, 1, 3, 2).reshape(NS * 32, HC)

    def weights(fc1, fc2, s_f, s_self, v_f, v_self, alpha, l2s, l2v):
        t = np.zeros((P, C_END), np.float32)
        for k in range(8):
            r = 16 * k
            t[r:r + fc1.shape[0], C_FC1 + 64 * (k % 2):C_FC1 + 64 * (k % 2) + 64] = fc1
        for k in range(2):
            t[64 * k:64 * k + 64, C_FC2:C_FC2 + 192] = fc2
        t[0:S0, C_A:C_A + S0] = s_f
        t[0:S0, C_A + S0:C_A + 2 * S0] = s_self
        for m in range(3):
            r, c = slice(V1 * m, V1 * m + V1), C_B + V1 * m
            t[r, c:c + V1] = v_f
            t[r, c + VF:c + VF + V1] = v_self
        t[VF, C_S] = 1.0
        t[0:VF, C_S + 1:C_S + 2] = alpha
        t[0:VF, C_S + 2:C_S + 66] = l2s
        t[0:VF, C_V:C_V + V1] = l2v
        return t

    w = {k: np.asarray(v) for k, v in w.items()}
    wts0 = weights(w["L0_gnn_Wfc1"], w["L0_gnn_Wfc2"], w["L0_gnn_Wl1_0"], w["L0_gnn_Wsc0"], w["L0_gnn_Wl1_1"],
                   w["L0_gnn_Wsc1"], w["L0_gnn_Wa"], w["L0_gnn_Wl2_s"], w["L0_gnn_Wl2_v"])
    wts1 = weights(w["L1_gnn_fcW1"], w["L1_gnn_fcW2"], w["L1_gnn_W1_s"], w["L1_gnn_W_sc_s"], w["L1_gnn_W1_v"],
                   w["L1_gnn_W_sc_v"], w["L1_gnn_W3"], w["L1_gnn_W2_s"], w["L1_gnn_W2_v"])

    nc = bacc.Bacc("TRN2", target_bir_lowering=False, num_devices=1)
    arrays, args = {}, []
    for name, a in (("x_nodes", x_m), ("x_t", x_t), ("src_t", src_t), ("sh_t", sh_t), ("es0_t", radial(edge_attr_16)),
                    ("es1_t", radial(edge_attr_8)), ("dst_t", dst_t), ("dst_rows", dst_rows),
                    ("attr", np.asarray(node_vec1)), ("wts0", wts0), ("wts1", wts1)):
        a = np.ascontiguousarray(a)
        arrays[name] = a
        args.append(nc.dram_tensor(name, a.shape, mybir.dt.from_np(a.dtype), kind="ExternalInput").ap())
    args.append(nc.dram_tensor("ftab", (N, D), mybir.dt.float32, kind="Internal").ap())
    args.append(nc.dram_tensor("nodes_out", (N, D), mybir.dt.float32, kind="ExternalOutput").ap())
    gnn(nc, *args)
    r = run_bass_kernel_spmd(nc, [arrays], core_ids=[0])
    y = r.results[0]["nodes_out"]
    return np.concatenate([y[:, :S0], y[:, S0:].reshape(N, 3, V1).transpose(0, 2, 1).reshape(N, VF)], axis=1)
```

```python
import math
from contextlib import ExitStack

import concourse.bass as bass
from concourse import mybir

N, D = 3125, 160
E = 100000
S0, V1 = 64, 32
VF = 3 * V1
NT = 25
NP = N // NT
P = 128
U = 4
SE = U * P
NS = -(-E // SE)
NB = NS // 4
assert NS % 4 == 0
WIN = 97
WX = 64
WX_SHIFT = 6
CH = VF + 1
NPAD = -(-(N + WIN) // 32) * 32
GT = 5
NG = NT // GT
HC = SE // 2
WCOL = 256

C_FC1 = 0
C_FC2 = C_FC1 + 128
C_A = C_FC2 + 192
C_B = C_A + 2 * S0
C_S = C_B + 2 * VF
C_V = C_S + 2 + S0
C_END = C_V + V1

PI_HI = 3.140625
PI_MID = math.floor((math.pi - PI_HI) * 2 ** 20) / 2 ** 20
PI_LO = math.pi - PI_HI - PI_MID
ROUND = 1.5 * 2 ** 23
FC_SCALE = (1.0 / math.sqrt(16), 1.0 / math.sqrt(8))
NODE = (14, 9)
ANGLE, REDUCED = 21, 10
ZC = 2 + D
BANKS = ((0, 3), (3, 2))
TR_BANK = (2, 6)
PROD_BANK = (4, 5, 2, 3, 6)


def gnn(nc, x_nodes, x_t, src_t, sh_t, es0_t, es1_t, dst_t, dst_rows, attr, wts0, wts1, ftab, out):
    fp32, i32 = mybir.dt.float32, mybir.dt.int32
    ALU, ACT, AX = mybir.AluOpType, mybir.ActivationFunctionType, mybir.AxisListType
    ds = bass.ds
    es_t = [es0_t, es1_t]
    ctx = ExitStack()
    with ctx:
        def sb(name, shape, dt=fp32):
            return ctx.enter_context(nc.sbuf_tensor(name, shape, dt))

        def sem(name):
            return ctx.enter_context(nc.semaphore(name))

        wts = [sb(f"w_sb{l}", [P, C_END]) for l in range(2)]
        ident = sb("ident", [P, P])
        iota_i = sb("iota_i", [P, WIN], i32)
        iota = sb("iota", [P, WIN])
        ones_row = sb("ones_row", [1, P])
        a_sb = sb("a_sb", [NP, NT])
        a2 = sb("a2", [NP, NT])
        a_ang = sb("a_ang", [NP, NT])
        a_conv = sb("a_conv", [NP, NT])
        dst_i = sb("dst_i", [P, NS * U], i32)
        rel = sb("rel", [P, 2, NS * U])
        rows_i = sb("rows_i", [NS // 2, 2, SE], i32)
        lo_hi = sb("lo_hi", [NS // 2, 2, 2], i32)
        more = sb("more", [NS // 2, 2, 2], i32)
        base_i = sb("base_i", [1, NS], i32)
        more_i = sb("more_i", [1, NS], i32)
        base_f = sb("base_f", [1, NS])
        more_f = sb("more_f", [1, NS])
        zero_f = sb("zero_f", [1, NS])
        extra_at = sb("extra_at", [1, NS + 4], i32)
        body_row = sb("body_row", [1, 8 * (NB + 1)], i32)
        X = sb("X", [NP, NT, D])
        FY = sb("FY", [NP, 2, NT, D])
        Z = sb("Z", [NP, NT, 2 + D])
        acc = sb("acc", [CH, 4, NPAD])
        xT = sb("xT", [VF, GT, 2, NP])
        stage = sb("stage", [CH, GT, 4, NP])
        v_g = sb("v_g", [NP, GT, D])
        sq_g = sb("sq_g", [NP, GT, D])
        xn_g = sb("xn_g", [NP, GT, D])
        small = sb("small", [NP, 8, GT])
        ang = sb("ang", [NP, 9, GT])
        c_self = sb("c_self", [NP, NT])
        c_conv = sb("c_conv", [NP, NT])
        idx = sb("idx", [P, 2, 2 * U], i32)
        sh = sb("sh", [P, 2, 2 * U, 4])
        es = sb("es", [P, HC])
        e_src = sb("e_src", [P, 4, U, D])
        e_sh0 = sb("e_sh0", [P, 2, U, D])
        sig = sb("sig", [P, 2, HC])
        hT = sb("hT", [P, 2, HC])
        em = sb("em", [P, U, 3, V1])
        t1 = sb("t1", [P, U, V1])
        t2 = sb("t2", [P, 2, U, V1])
        p1 = sb("p1", [P, 2, U, S0])
        msg = sb("msg", [P, 2, U, 4, CH])
        hot = sb("hot", [P, 2, U, WIN])
        hot_x = sb("hot_x", [P, U, WX])
        PS = ctx.enter_context(nc.psum_tensor("PS", [P, 8, 512], fp32))

        def h_ps(k):
            return PS[:, k, 0:HC]

        rows_01, rows_23 = [e_src[:, 2 * j:2 * j + 2, :, :].rearrange("p q u d -> p (q u d)")[:, 0:2 * GT * NP]
                            .rearrange("p (k c n) -> p k c n", k=GT, c=2) for j in range(2)]
        x_cols = [xT, stage[:, :, 0:2, :], stage[:, :, 2:4, :], rows_01, rows_23]

        def w_ps(k):
            return PS[:, 2 + 2 * k:4 + 2 * k, :].rearrange("p b (j c) -> p (b j) c", c=WCOL)

        def s_ps(k):
            return PS[0:CH, 6 + k, 0:4 * WIN].rearrange("p (c w) -> p c w", w=WIN)

        def small_row(j):
            return small[:, j, :]

        f_sum, sq_sum, neg_mean, var, dev, inv_dev, n_a, n_b = [small_row(j) for j in range(8)]
        angle, rounded, quot, rest, sign_a, sign_b, sign, sin_r, sin_half = [ang[:, j, :] for j in range(9)]

        s_const = sem("s_const")
        s_wts = [sem(f"s_wts{l}") for l in range(2)]
        s_attr = sem("s_attr")
        s_xld = sem("s_xld")
        s_dst = sem("s_dst")
        s_rows = sem("s_rows")
        s_lohi = sem("s_lohi")
        s_tab = sem("s_tab")
        s_setup = sem("s_setup")
        s_wready = sem("s_wready")
        s_agg = sem("s_agg")
        s_basef = sem("s_basef")
        s_bb = sem("s_bb")
        s_xtab = sem("s_xtab")
        s_acc0 = sem("s_acc0")
        s_xT = [sem(f"s_xT{g}") for g in range(NG)]
        s_pre = sem("s_pre")
        s_f = sem("s_f")
        s_ftab = sem("s_ftab")
        s_tr = sem("s_tr")
        s_trc = sem("s_trc")
        s_idx = [sem(f"s_idx{k}") for k in range(2)]
        s_sh = [sem(f"s_sh{k}") for k in range(2)]
        s_es = [sem(f"s_es{k}") for k in range(2)]
        s_gath = [sem(f"s_gath{k}") for k in range(4)]
        s_go = sem("s_go")
        s_h = sem("s_h")
        s_sig = sem("s_sig")
        s_hT = sem("s_hT")
        s_w = sem("s_w")
        s_esh = sem("s_esh")
        s_em = sem("s_em")
        s_t1 = sem("s_t1")
        s_t2 = sem("s_t2")
        s_p1 = sem("s_p1")
        s_wfree = sem("s_wfree")
        s_msg = sem("s_msg")
        s_n2 = sem("s_n2")
        s_scat = sem("s_scat")
        s_acc = sem("s_acc")
        s_xrel = [sem(f"s_xrel{l}") for l in range(2)]
        s_xhot = [sem(f"s_xhot{l}") for l in range(2)]
        s_xscat = [sem(f"s_xscat{l}") for l in range(2)]
        s_xadd = [sem(f"s_xadd{l}") for l in range(2)]
        s_stage = sem("s_stage")
        s_conv = sem("s_conv")
        s_z = sem("s_z")
        s_node = sem("s_node")
        s_angle = sem("s_angle")
        s_self = sem("s_self")
        s_sin = sem("s_sin")
        s_sq = sem("s_sq")
        s_cen = sem("s_cen")
        s_sqrt = sem("s_sqrt")
        s_xn = sem("s_xn")
        s_xcopy = sem("s_xcopy")
        s_out = sem("s_out")

        block = ctx.enter_context(nc.Block())
        out_v = out.rearrange("(p i) f -> p (i f)", i=NT)
        ftab_v = ftab.rearrange("(p i) f -> p (i f)", i=NT)
        x_v = x_nodes.rearrange("(p i) f -> p i f", i=NT)
        xs_v = x_t[0:S0, :].rearrange("f (g n) -> f g n", g=NG)
        xv_v = x_t[S0:D, :].rearrange("f (g n) -> f g n", g=NG)

        @block.sync
        def _(sp):
            def load_x_cols(g):
                for part, view, rows in ((0, xs_v, S0), (1, xv_v, VF)):
                    sp.dma_start(x_cols[g][0:rows, :, part, :],
                                 view[:, g, :].rearrange("f (k n) -> f k n", n=NP)).then_inc(s_xT[g], 16)

            sp.dma_start(wts[0][:, :], wts0).then_inc(s_wts[0], 16)
            load_x_cols(0)
            sp.dma_start(a_sb[:, :], attr.rearrange("(p i) o -> p (i o)", i=NT)).then_inc(s_attr, 16)
            load_x_cols(1)
            sp.dma_start(rows_i[:, :, :], dst_rows).then_inc(s_rows, 16)
            load_x_cols(2)
            sp.dma_start(dst_i[:, :], dst_t).then_inc(s_dst, 16)
            load_x_cols(3)
            load_x_cols(4)
            sp.dma_start(wts[1][:, :], wts1).then_inc(s_wts[1], 16)
            sp.wait_ge(s_lohi, 1)
            sp.dma_start(base_i[0:1, :], more[:, 0, :]).then_inc(s_tab, 16)
            sp.dma_start(more_i[0:1, :], more[:, 1, :]).then_inc(s_tab, 16)

            def load_half(l, b, half, first):
                B = NB * l + b
                if not first:
                    sp.wait_ge(s_gath[2 * half], 64 * B)
                    sp.wait_ge(s_gath[2 * half + 1], 64 * B)
                sp.dma_start(idx[:, half, :], src_t[:, ds((b * 2 + half) * 2 * U, 2 * U)]).then_inc(s_idx[half], 16)
                if not first:
                    sp.wait_ge(s_tab, 32)
                    sp.wait_ge(s_msg, 4 * B + 2 * half - 2)
                    sp.wait_ge(s_n2, 4 * B + 2 * half - 2)
                sp.dma_start(sh[:, half, :, :].rearrange("p k c -> p (k c)"),
                             sh_t[:, ds((b * 2 + half) * 2 * U * 4, 2 * U * 4)]).then_inc(s_sh[half], 16)

            def load_es(l, b, half, first):
                B = NB * l + b
                if not first:
                    sp.wait_ge(s_h, 4 * B + 2 * half - 2)
                sp.dma_start(es[64 * half:64 * half + 64, :], es_t[l][ds((b * 2 + half) * 64, 64), :]).then_inc(s_es[half], 16)

            def first_loads(l):
                for half in range(2):
                    load_es(l, 0, half, l == 0)
                    load_half(l, 0, half, l == 0)

            def layer_loads(l):
                with sp.Fori(1, NB) as b:
                    for half in range(2):
                        load_es(l, b, half, False)
                        load_half(l, b, half, False)

            def table_out(l, g):
                sp.wait_ge(s_f, NT * l + GT * (g + 1))
                sp.dma_start(ftab_v[:, ds(GT * D * g, GT * D)],
                             FY[:, 0, ds(GT * g, GT), :].rearrange("p i f -> p (i f)")).then_inc(s_ftab, 16)

            first_loads(0)
            with sp.Fori(0, NG) as g:
                table_out(0, g)
            sp.dma_start(X[:, :, :], x_v).then_inc(s_xld, 16)
            layer_loads(0)
            with sp.Fori(0, NG) as g:
                table_out(1, g)
            first_loads(1)
            layer_loads(1)
            with sp.Fori(0, NG) as g:
                sp.wait_ge(s_xn, NG + g + 1)
                sp.dma_start(out_v[:, ds(GT * D * g, GT * D)],
                             X[:, ds(GT * g, GT), :].rearrange("p i f -> p (i f)")).then_inc(s_out, 16)
            sp.wait_ge(s_out, 16 * NG)

        @block.gpsimd
        def _(pool):
            pool.memset(ident[:, :], 0.0).then_inc(s_const, 1)
            pool.iota(iota_i[:, :], pattern=[[1, WIN]], base=0, channel_multiplier=0).then_inc(s_const, 1)
            pool.memset(msg[:, :, :, :, VF:CH], 1.0).then_inc(s_const, 1)
            pool.memset(ones_row[:, :], 1.0).then_inc(s_const, 1)
            pool.wait_ge(s_const, 4)
            pool.affine_select(out=ident[:, :], in_=ident[:, :], compare_op=ALU.not_equal, fill=1.0,
                               base=0, pattern=[[-1, P]], channel_multiplier=1).then_inc(s_const, 1)
            pool.memset(acc[:, :, :], 0.0).then_inc(s_acc0, 1)

            def gather_body(l, b, first):
                B = NB * l + b
                for q in range(4):
                    half = q // 2
                    pool.wait_ge(s_ftab, 16 * NG * (l + 1))
                    if q % 2 == 0:
                        pool.wait_ge(s_idx[half], 16 * (B + 1))
                    if not first:
                        pool.wait_ge(s_msg, 4 * B + q - 3)
                        pool.wait_ge(s_esh, 4 * B + q - 3)
                    pool.sem_inc(s_go, 1)
                    for u in range(U):
                        k = (q % 2) * U + u
                        pool.indirect_dma_start(out=e_src[:, q, u, :], out_offset=None, in_=ftab,
                                                in_offset=bass.IndirectOffsetOnAxis(ap=idx[:, half, k:k + 1], axis=0)
                                                ).then_inc(s_gath[q], 16)

            def keep_rows(g):
                pool.wait_ge(s_xn, g + 1)
                pool.tensor_copy(X[:, ds(GT * g, GT), :], xn_g[:, :, :]).then_inc(s_xcopy, 1)

            def angles(g):
                step = [0]

                def then(ins):
                    step[0] += 1
                    ins.then_inc(s_angle, 1)
                    pool.wait_ge(s_angle, ANGLE * g + step[0])
                    pool.sem_inc(s_go, 1)

                alpha = Z[:, ds(GT * g, GT), 1:2].rearrange("p i a -> p (i a)")
                pool.wait_ge(s_z, 2 * (NG + g + 1))
                then(pool.tensor_tensor(angle, alpha, a_ang[:, ds(GT * g, GT)], ALU.mult))
                then(pool.tensor_scalar(rounded, angle, 1.0 / math.pi, ROUND, ALU.mult, ALU.add))
                then(pool.tensor_scalar(quot, rounded, ROUND, None, ALU.subtract))
                then(pool.tensor_scalar(sign_a, quot, -PI_HI, None, ALU.mult))
                then(pool.tensor_tensor(rest, angle, sign_a, ALU.add))
                then(pool.tensor_scalar(sign_a, quot, -PI_MID, None, ALU.mult))
                then(pool.tensor_tensor(rest, rest, sign_a, ALU.add))
                then(pool.tensor_scalar(sign_a, quot, -PI_LO, None, ALU.mult))
                then(pool.tensor_tensor(rest, rest, sign_a, ALU.add))
                then(pool.tensor_scalar(rest, rest, -3.1415925, 3.1415925, ALU.max, ALU.min))
                assert step[0] == REDUCED
                then(pool.tensor_scalar(sign_a, quot, 0.5, ROUND, ALU.mult, ALU.add))
                then(pool.tensor_scalar(sign_b, sign_a, ROUND, None, ALU.subtract))
                then(pool.tensor_scalar(sign_a, sign_b, -2.0, None, ALU.mult))
                then(pool.tensor_tensor(sign_a, sign_a, quot, ALU.add))
                then(pool.tensor_tensor(sign_b, sign_a, sign_a, ALU.mult))
                then(pool.tensor_scalar(sign, sign_b, -2.0, 1.0, ALU.mult, ALU.add))
                pool.wait_ge(s_sin, g + 1)
                pool.sem_inc(s_go, 1)
                then(pool.tensor_tensor(sign_a, sin_half, sin_half, ALU.mult))
                then(pool.tensor_scalar(sign_a, sign_a, -2.0, 1.0, ALU.mult, ALU.add))
                then(pool.tensor_tensor(c_self[:, ds(GT * g, GT)], sign_a, sign, ALU.mult))
                then(pool.tensor_tensor(sign_b, sin_r, sign, ALU.mult))
                then(pool.tensor_tensor(c_conv[:, ds(GT * g, GT)], sign_b, a_conv[:, ds(GT * g, GT)], ALU.mult))
                assert step[0] == ANGLE

            for l in range(2):
                gather_body(l, 0, l == 0)
                with pool.Fori(1, NB) as b:
                    gather_body(l, b, False)
                if l == 0:
                    with pool.Fori(0, NG - 1) as g:
                        keep_rows(g)
                    pool.wait_ge(s_stage, NG)
                    pool.memset(acc[:, :, :], 0.0).then_inc(s_acc0, 1)
                    keep_rows(NG - 1)
            with pool.Fori(0, NG) as g:
                angles(g)

        @block.scalar
        def _(act):
            def gate(l, T, k):
                act.wait_ge(s_h, T + 1)
                if not (isinstance(T, int) and T < 2):
                    act.wait_ge(s_hT, T - 1)
                act.activation(sig[:, k, :], h_ps(k), ACT.Sigmoid, scale=FC_SCALE[l]).then_inc(s_sig, 1)

            def edge_body(l, b, last):
                B = NB * l + b
                for q in range(4):
                    T = 4 * B + q
                    half, k = q // 2, q % 2
                    if not (last and q == 3):
                        gate(l, T + 1, 1 - k)
                    act.wait_ge(s_gath[q], 64 * (B + 1))
                    if k == 0:
                        act.wait_ge(s_sh[half], 16 * (B + 1))
                    if not (isinstance(T, int) and T < 2):
                        act.wait_ge(s_wfree, T - 1)
                    for u in range(U):
                        ins = act.activation(e_sh0[:, k, u, :], e_src[:, q, u, :], ACT.Copy,
                                             scale=sh[:, half, k * U + u, 0:1])
                    ins.then_inc(s_esh, 1)
                    act.wait_ge(s_p1, T + 1)
                    for u in range(U):
                        for m in range(1, 3):
                            ins = act.activation(msg[:, k, u, 1 + m, 0:S0], p1[:, k, u, :], ACT.Copy,
                                                 scale=sh[:, half, k * U + u, 1 + m:2 + m])
                    ins.then_inc(s_n2, 1)

            def table_out_of_psum(l, g):
                for k in range(GT):
                    i = GT * g + k
                    act.wait_ge(s_pre, NT * l + i + 1)
                    bank = PS[0:NP, PROD_BANK[k], :]
                    act.activation(FY[:, :, ds(i, 1), 0:S0].rearrange("p j a f -> p j (a f)"),
                                   bank[:, 0:2 * S0].rearrange("p (j f) -> p j f", j=2), ACT.Copy, scale=a_sb[:, ds(i, 1)])
                    act.activation(FY[:, :, ds(i, 1), S0:D].rearrange("p j a f -> p j (a f)"),
                                   bank[:, 2 * S0:2 * D].rearrange("p (j f) -> p j f", j=2), ACT.Copy,
                                   scale=a_sb[:, ds(i, 1)]).then_inc(s_f, 1)

            def stage_group(l, g):
                by_tile = acc[:, :, 0:N].rearrange("q c (p i) -> q c i p", i=NT)
                act.activation(stage[:, :, :, :].rearrange("q k c p -> q c k p"), by_tile[:, :, ds(GT * g, GT), :],
                               ACT.Copy).then_inc(s_stage, 1)

            def conv_out(l, g):
                for j, (k, n) in enumerate(BANKS):
                    act.wait_ge(s_conv, 2 * (NG * l + g) + j + 1)
                    act.activation(Z[:, ds(GT * g + k, n), :],
                                   PS[0:NP, j, 0:n * ZC].rearrange("p (i f) -> p i f", f=ZC), ACT.Copy).then_inc(s_z, 1)

            def sines(g):
                act.wait_ge(s_angle, ANGLE * g + REDUCED)
                act.activation(sin_r, rest, ACT.Sin)
                act.activation(sin_half, rest, ACT.Sin, scale=0.5).then_inc(s_sin, 1)

            def self_scaled(g):
                act.wait_ge(s_angle, ANGLE * (g + 1))
                for k in range(GT):
                    ins = act.activation(sq_g[:, k, :], FY[:, 1, ds(GT * g + k, 1), :].rearrange("p a f -> p (a f)"),
                                         ACT.Copy, scale=c_self[:, ds(GT * g + k, 1)])
                ins.then_inc(s_self, 1)

            def squares(l, g):
                act.wait_ge(s_cen, NG * l + g + 1)
                for k in range(GT):
                    ins = act.activation((sq_g, xn_g)[l][:, k, :], v_g[:, k, :], ACT.Square,
                                         bias=neg_mean[:, k:k + 1], accum_out=sq_sum[:, k:k + 1])
                ins.then_inc(s_sq, 1)

            def deviation(l, g):
                act.wait_ge(s_node, NODE[0] * NG * l + NODE[l] * (g + 1) - 5)
                act.activation(dev, var, ACT.Sqrt).then_inc(s_sqrt, 1)

            def node_group_0(g, left):
                deviation(0, g)
                if left >= 1:
                    conv_out(0, g + 1)
                if left >= 2:
                    stage_group(0, g + 2)
                for j, (k, n) in enumerate(BANKS):
                    act.wait_ge(s_tr, 2 * g + j + 1)
                    for part, rows in ((0, S0), (1, VF)):
                        ins = act.activation(xT[0:rows, k:k + n, part, :],
                                             PS[0:rows, TR_BANK[j] + part, 0:n * NP].rearrange("f (k n) -> f k n", n=NP),
                                             ACT.Copy)
                    ins.then_inc(s_trc, 1)
                table_out_of_psum(1, g)
                if left >= 1:
                    squares(0, g + 1)

            def node_group_1(g, left):
                deviation(1, g)
                if left >= 1:
                    self_scaled(g + 1)
                if left >= 2:
                    conv_out(1, g + 2)
                if left >= 3:
                    stage_group(1, g + 3)
                if left >= 2:
                    sines(g + 2)
                if left >= 1:
                    squares(1, g + 1)

            act.wait_ge(s_attr, 16)
            table_out_of_psum(0, 0)
            with act.Fori(1, NG) as g:
                table_out_of_psum(0, g)
            for l in range(2):
                gate(l, NS * l, 0)
                edge_body(l, 0, False)
                with act.Fori(1, NB - 1) as b:
                    edge_body(l, b, False)
                edge_body(l, NB - 1, True)
                act.wait_ge(s_agg, l + 1)
                stage_group(l, 0)
                conv_out(l, 0)
                stage_group(l, 1)
                if l == 0:
                    squares(0, 0)
                    with act.Fori(0, NG - 2) as g:
                        node_group_0(g, 2)
                    node_group_0(NG - 2, 1)
                    node_group_0(NG - 1, 0)
                else:
                    sines(0)
                    self_scaled(0)
                    conv_out(1, 1)
                    stage_group(1, 2)
                    sines(1)
                    squares(1, 0)
                    with act.Fori(0, NG - 3) as g:
                        node_group_1(g, 3)
                    for left in range(2, -1, -1):
                        node_group_1(NG - 1 - left, left)

        @block.vector
        def _(vec):
            done = [0]

            def then(ins):
                done[0] += 1
                ins.then_inc(s_setup, 1)
                vec.wait_ge(s_setup, done[0])

            def scale_weights(l):
                vec.wait_ge(s_wts[l], 16)
                for sl, c in ((wts[l][0:S0, C_A:C_A + S0], 1.0 / 64), (wts[l][0:S0, C_A + S0:C_A + 2 * S0], 1.0 / 8),
                              (wts[l][0:VF, C_B:C_B + VF], 1.0 / (8 * math.sqrt(32))),
                              (wts[l][0:VF, C_B + VF:C_B + 2 * VF], 1.0 / math.sqrt(32)),
                              (wts[l][S0:VF, C_S:C_S + 66], 1.0 / math.sqrt(3))):
                    vec.tensor_scalar(sl, sl, c, None, ALU.mult).then_inc(s_wready, 1)

            scale_weights(0)
            vec.wait_ge(s_rows, 16)
            vec.tensor_reduce(more[:, 0, :], rows_i[:, :, :], AX.X, ALU.min)
            then(vec.tensor_reduce(lo_hi[:, 1, :], rows_i[:, :, :], AX.X, ALU.max))
            then(vec.tensor_tensor(lo_hi[:, 0, :], lo_hi[:, 1, :], more[:, 0, :], ALU.subtract))
            then(vec.tensor_scalar(lo_hi[:, 1, :], lo_hi[:, 0, :], WX - WIN, 0, ALU.add, ALU.max))
            vec.tensor_scalar(more[:, 1, :], lo_hi[:, 1, :], WX_SHIFT, None, ALU.arith_shift_right).then_inc(s_lohi, 1)
            vec.wait_ge(s_attr, 16)
            vec.tensor_scalar(a_ang[:, :], a_sb[:, :], 0.1 / math.sqrt(960), None, ALU.mult)
            vec.tensor_scalar(a_conv[:, :], a_sb[:, :], 1.0 / math.sqrt(960), None, ALU.mult)
            then(vec.tensor_tensor(a2[:, :], a_sb[:, :], a_sb[:, :], ALU.mult))
            then(vec.tensor_scalar(a2[:, :], a2[:, :], 1.0 / 96, None, ALU.mult))
            vec.memset(extra_at[:, :], 0)
            vec.memset(body_row[:, :], 0)
            vec.memset(zero_f[:, :], 0.0)
            vec.wait_ge(s_const, 5)
            then(vec.tensor_copy(iota[:, :], iota_i[:, :]))
            vec.wait_ge(s_tab, 32)
            vec.tensor_copy(base_f[:, :], base_i[:, :]).then_inc(s_basef, 1)
            then(vec.tensor_copy(more_f[:, :], more_i[:, :]))
            vec.tensor_tensor_scan(extra_at[0:1, 1:NS + 1], more_f[:, :], zero_f[:, :], 0.0, ALU.add,
                                   ALU.add).then_inc(s_xtab, 1)
            rows = body_row[0:1, :].rearrange("p (b c) -> p b c", c=8)
            by_body = base_i[0:1, :].rearrange("p (b q) -> p b q", q=4)
            extra_by_body = extra_at[0:1, 0:NS].rearrange("p (b q) -> p b q", q=4)
            vec.tensor_copy(rows[:, 0:NB, 1:4], by_body[:, :, 0:3])
            vec.tensor_copy(rows[:, 1:NB + 1, 0:1], by_body[:, :, 3:4])
            vec.wait_ge(s_xtab, 1)
            vec.tensor_copy(rows[:, 0:NB, 5:6], extra_by_body[:, :, 3:4])
            vec.tensor_copy(rows[:, 0:NB, 6:7], extra_by_body[:, :, 0:1])
            vec.tensor_copy(rows[:, 1:NB + 1, 4:5], extra_by_body[:, :, 3:4])
            vec.tensor_copy(rows[:, 0:NB, 7:8], extra_at[0:1, 4:NS + 4].rearrange("p (b q) -> p b q", q=4)[:, :, 0:1])\
                .then_inc(s_xtab, 1)
            vec.wait_ge(s_bb, 1)
            vec.wait_ge(s_dst, 16)
            for l in range(2):
                ins = vec.tensor_tensor(rel[:, l, :].rearrange("p (s u) -> p s u", u=U),
                                        dst_i[:, :].rearrange("p (s u) -> p s u", u=U),
                                        PS[:, 7, 0:NS].unsqueeze(2).broadcast_to([P, NS, U]), ALU.subtract)
            then(ins)
            vec.wait_ge(s_xtab, 2)
            scale_weights(1)

            def add_window(k, at, width):
                part = acc[:, :, ds(at, width)]
                return vec.tensor_tensor(part, part, s_ps(k)[:, :, 0:width], ALU.add)

            def is_hot(out_hot, l, s, first, width):
                return vec.tensor_tensor(out_hot, rel[:, l, ds(U * s, U)].unsqueeze(2).broadcast_to([P, U, width]),
                                         iota[:, first:first + width].unsqueeze(1).broadcast_to([P, U, width]),
                                         ALU.is_equal)

            row_regs = [vec.alloc_register(f"v_row{j}") for j in range(6)]

            def row_of(b):
                vec.load(row_regs, body_row[0:1, ds(8 * b, 6)])
                return ([vec.snap(r, min_val=0, max_val=N - 1) for r in row_regs[0:4]]
                        + [vec.snap(r, min_val=0, max_val=NS * 49) for r in row_regs[4:6]])

            def extra_before(s):
                return vec.value_load(extra_at[0:1, ds(s, 1)], min_val=0, max_val=NS * 49)

            def add_up(l, s, k, base):
                T = NS * l + s
                vec.wait_ge(s_scat, T + 1)
                if not (isinstance(T, int) and T == 0):
                    vec.wait_ge(s_acc, T)
                add_window(k, base, WIN).then_inc(s_acc, 1)

            def add_further(l, s, k, base):
                T = NS * l + s
                v0, v1 = extra_before(s), extra_before(s + 1)
                with vec.If(v1 > v0):
                    with vec.Fori(v0, v1) as v:
                        vec.wait_ge(s_acc, T + 1)
                        part = rel[:, l, ds(U * s, U)]
                        vec.tensor_scalar(part, part, float(WX), None, ALU.subtract).then_inc(s_xrel[l], 1)
                        vec.wait_ge(s_xrel[l], v + 1)
                        is_hot(hot_x[:, :, :], l, s, WIN - WX, WX).then_inc(s_xhot[l], 1)
                        vec.wait_ge(s_xscat[l], v + 1)
                        at = nc.s_assert_within(base + WX * (v - v0) + WIN, 0, NPAD - WX,
                                                skip_runtime_bounds_check_because="it is at most the largest dst")
                        add_window(k, at, WX).then_inc(s_xadd[l], 1)
                        vec.wait_ge(s_xadd[l], v + 1)

            def sh_of(q):
                return sh[:, q // 2, (q % 2) * U:(q % 2) * U + U, :]

            def hidden(l, T, k):
                vec.wait_ge(s_sig, T + 1)
                vec.scalar_tensor_tensor(out=hT[:, k, :], in0=h_ps(k), scalar=FC_SCALE[l], in1=sig[:, k, :],
                                         op0=ALU.mult, op1=ALU.mult).then_inc(s_hT, 1)

            def vector_rows(T, q, B):
                vec.wait_ge(s_gath[q], 64 * (B + 1))
                if q % 2 == 0:
                    vec.wait_ge(s_sh[q // 2], 16 * (B + 1))
                vec.tensor_tensor(em[:, :, :, :], e_src[:, q, :, S0:D].rearrange("p u (m v) -> p u m v", v=V1),
                                  sh_of(q)[:, :, 1:4].unsqueeze(3).broadcast_to([P, U, 3, V1]),
                                  ALU.mult).then_inc(s_em, 1)

            def rows_summed(l, s, T, k):
                vec.wait_ge(s_em, T + 1)
                vec.tensor_tensor(t1[:, :, :], em[:, :, 0, :], em[:, :, 1, :], ALU.add).then_inc(s_t1, 1)
                is_hot(hot[:, k, :, :], l, s, 0, WIN)
                vec.wait_ge(s_t1, T + 1)
                vec.tensor_tensor(t2[:, k, :, :], t1[:, :, :], em[:, :, 2, :], ALU.add).then_inc(s_t2, 1)

            def edge_body(l, b, first, last):
                *base, before, after = row_of(b)
                with vec.If(after > before):
                    edge_steps(l, b, first, last, base, True)
                with vec.Else():
                    edge_steps(l, b, first, last, base, False)

            def edge_steps(l, b, first, last, base, further):
                B = NB * l + b
                for q in range(4):
                    s, T = 4 * b + q, 4 * B + q
                    k = q % 2
                    w = w_ps(k)
                    out_m = msg[:, k, :, :, :]
                    if not (last and q == 3):
                        hidden(l, T + 1, 1 - k)
                    vec.wait_ge(s_w, T + 1)
                    vec.tensor_tensor(p1[:, k, :, :], w[:, :, 64:128], e_src[:, q, :, 0:S0], ALU.mult).then_inc(s_p1, 1)
                    vec.wait_ge(s_esh, T + 1)
                    vec.tensor_tensor(out_m[:, :, 0, 0:S0], w[:, :, 0:64], e_sh0[:, k, :, 0:S0], ALU.mult)
                    vec.tensor_tensor(out_m[:, :, 1:4, S0:VF],
                                      w[:, :, 128:160].unsqueeze(2).broadcast_to([P, U, 3, V1]),
                                      e_sh0[:, k, :, S0:D].rearrange("p u (m v) -> p u m v", v=V1), ALU.mult)
                    vec.wait_ge(s_t2, T + 1)
                    vec.tensor_tensor(out_m[:, :, 0, S0:VF], w[:, :, 160:192], t2[:, k, :, :],
                                      ALU.mult).then_inc(s_wfree, 1)
                    vec.wait_ge(s_p1, T + 1)
                    vec.tensor_tensor(out_m[:, :, 1, 0:S0], p1[:, k, :, :],
                                      sh_of(q)[:, :, 1:2].broadcast_to([P, U, S0]), ALU.mult).then_inc(s_msg, 1)
                    if not (last and q == 3):
                        vector_rows(T + 1, (q + 1) % 4, B + (q + 1) // 4)
                    if not (first and q == 0):
                        add_up(l, s - 1, 1 - k, base[q])
                    if not (last and q == 3):
                        rows_summed(l, s + 1, T + 1, 1 - k)
                    if further and not (first and q == 0):
                        add_further(l, s - 1, 1 - k, base[q])

            def node_group(l, g):
                first_step = NODE[0] * NG * l + NODE[l] * g
                step = [0]

                def then(ins):
                    step[0] += 1
                    ins.then_inc(s_node, 1)
                    vec.wait_ge(s_node, first_step + step[0])

                z = Z[:, ds(GT * g, GT), :]
                if l == 0:
                    vec.wait_ge(s_z, 2 * (g + 1))
                    alpha = z[:, :, 1:2].rearrange("p i a -> p (i a)")
                    count = z[:, :, 0:1].rearrange("p i a -> p (i a)")
                    then(vec.tensor_scalar(n_a, count, 1.0, None, ALU.max))
                    then(vec.reciprocal(n_b, n_a))
                    then(vec.tensor_tensor(n_a, alpha, n_b, ALU.mult))
                    then(vec.tensor_tensor(var, n_b, a2[:, ds(GT * g, GT)], ALU.mult))
                    then(vec.tensor_tensor(n_b, n_a, var, ALU.mult))
                else:
                    vec.wait_ge(s_angle, ANGLE * (g + 1))
                    vec.wait_ge(s_self, g + 1)
                if not (l == 0 and isinstance(g, int) and g == 0):
                    vec.wait_ge(s_xn, NG * l + g)
                for k in range(GT):
                    i = GT * g + k
                    factor = n_b[:, k:k + 1] if l == 0 else c_conv[:, ds(i, 1)]
                    self_con = FY[:, 1, ds(i, 1), :].rearrange("p a f -> p (a f)") if l == 0 else sq_g[:, k, :]
                    ins = vec.scalar_tensor_tensor(out=v_g[:, k, :], in0=Z[:, ds(i, 1), 2:ZC].rearrange("p a f -> p (a f)"),
                                                   scalar=factor, in1=self_con, op0=ALU.mult, op1=ALU.add)
                then(ins)
                vec.wait_ge(s_xld, 16)
                if l == 1:
                    vec.wait_ge(s_xcopy, NG)
                then(vec.tensor_tensor(v_g[:, :, :], v_g[:, :, :], X[:, ds(GT * g, GT), :], ALU.add))
                then(vec.tensor_reduce(f_sum, v_g[:, :, :], AX.X, ALU.add))
                vec.tensor_scalar(neg_mean, f_sum, -1.0 / D, None, ALU.mult).then_inc(s_cen, 1)
                vec.wait_ge(s_sq, NG * l + g + 1)
                then(vec.tensor_scalar(var, sq_sum, 1.0 / D, 1e-5, ALU.mult, ALU.add))
                vec.wait_ge(s_sqrt, NG * l + g + 1)
                then(vec.reciprocal(n_a, dev))
                then(vec.tensor_tensor(n_b, n_a, n_a, ALU.mult))
                then(vec.tensor_tensor(f_sum, n_b, var, ALU.mult))
                then(vec.tensor_scalar(n_b, f_sum, -0.5, 1.5, ALU.mult, ALU.add))
                then(vec.tensor_tensor(inv_dev, n_a, n_b, ALU.mult))
                if l == 0 and not (isinstance(g, int) and g == 0):
                    vec.wait_ge(s_xcopy, g)
                    vec.wait_ge(s_tr, 2 * g)
                for k in range(GT):
                    normed = xn_g[:, k, :] if l == 0 else X[:, ds(GT * g + k, 1), :].rearrange("p a f -> p (a f)")
                    ins = vec.tensor_scalar(normed, v_g[:, k, :], neg_mean[:, k:k + 1], inv_dev[:, k:k + 1],
                                            ALU.add, ALU.mult)
                ins.then_inc(s_xn, 1)
                assert step[0] == NODE[l]

            for l in range(2):
                vec.wait_ge(s_acc0, l + 1)
                T = NS * l
                hidden(l, T, 0)
                vector_rows(T, 0, NB * l)
                rows_summed(l, 0, T, 0)
                edge_body(l, 0, True, False)
                with vec.Fori(1, NB - 1) as b:
                    edge_body(l, b, False, False)
                edge_body(l, NB - 1, False, True)
                base = row_of(NB)[0]
                add_up(l, NS - 1, 1, base)
                add_further(l, NS - 1, 1, base)
                vec.wait_ge(s_acc, NS * (l + 1))
                vec.sem_inc(s_agg, 1)
                node_group(l, 0)
                with vec.Fori(1, NG) as g:
                    node_group(l, g)

        @block.tensor
        def _(pe):
            def hidden(l, T, q, B):
                if q % 2 == 0:
                    pe.wait_ge(s_es[q // 2], 16 * (B + 1))
                if not (isinstance(T, int) and T < 2):
                    pe.wait_ge(s_hT, T - 1)
                r = slice(32 * q, 32 * q + 32)
                pe.matmul(h_ps(q % 2), wts[l][r, C_FC1:C_FC1 + P], es[r, :], start=True, stop=True).then_inc(s_h, 1)

            def edge_weights(l, T, k):
                pe.wait_ge(s_hT, T + 1)
                if not (isinstance(T, int) and T < 2):
                    pe.wait_ge(s_wfree, T - 1)
                for u in (0, 2, 1, 3):
                    r = slice(64 * (u // 2), 64 * (u // 2) + 64)
                    ins = pe.matmul(w_ps(k)[:, u, 0:192], hT[r, k, (u % 2) * P:(u % 2) * P + P],
                                    wts[l][r, C_FC2:C_FC2 + 192], start=True, stop=True)
                ins.then_inc(s_w, 1)

            def sums(k, onehot, width):
                for c in range(4):
                    for u in range(U):
                        ins = pe.matmul(s_ps(k)[:, c, 0:width], msg[:, k, u, c, :], onehot[:, u, :],
                                        start=(u == 0), stop=(u == U - 1))
                return ins

            row_regs = [pe.alloc_register(f"t_row{j}") for j in range(2)]

            def extra_before(s):
                return pe.value_load(extra_at[0:1, ds(s, 1)], min_val=0, max_val=NS * 49)

            def edge_body(l, b, last):
                pe.load(row_regs, body_row[0:1, ds(8 * b + 6, 2)])
                before, after = [pe.snap(r, min_val=0, max_val=NS * 49) for r in row_regs]
                with pe.If(after > before):
                    edge_steps(l, b, last, True)
                with pe.Else():
                    edge_steps(l, b, last, False)

            def edge_steps(l, b, last, further):
                B = NB * l + b
                for q in range(4):
                    s, T = 4 * b + q, 4 * B + q
                    k = q % 2
                    if not (last and q >= 2):
                        hidden(l, T + 2, (q + 2) % 4, B + (q + 2) // 4)
                    if not (last and q == 3):
                        edge_weights(l, T + 1, 1 - k)
                    pe.wait_ge(s_msg, T + 1)
                    pe.wait_ge(s_n2, T + 1)
                    if not (isinstance(T, int) and T < 2):
                        pe.wait_ge(s_acc, T - 1)
                    sums(k, hot[:, k, :, :], WIN).then_inc(s_scat, 1)
                    if further:
                        v0, v1 = extra_before(s), extra_before(s + 1)
                        with pe.If(v1 > v0):
                            with pe.Fori(v0, v1) as v:
                                pe.wait_ge(s_xhot[l], v + 1)
                                sums(k, hot_x[:, :, :], WX).then_inc(s_xscat[l], 1)

            def node_products(l, g, cols):
                W = wts[l]
                for k in range(GT):
                    if l == 1:
                        pe.wait_ge(s_trc, 2 * g + (1 if k < BANKS[1][0] else 2))
                    elif g > 0:
                        pe.wait_ge(s_f, GT * (g - 1) + k + 1)
                    bank = PS[0:NP, PROD_BANK[k], :]
                    pe.matmul(bank[:, 0:2 * S0], cols[0:S0, k, 0, :], W[0:S0, C_A:C_A + 2 * S0], start=True, stop=True)
                    pe.matmul(bank[:, 2 * S0:2 * D], cols[0:VF, k, 1, :], W[0:VF, C_B:C_B + 2 * VF],
                              start=True, stop=True).then_inc(s_pre, 1)

            def conv_products(l, g):
                W = wts[l]
                pe.wait_ge(s_stage, NG * l + g + 1)
                if not (isinstance(g, int) and g == 0):
                    pe.wait_ge(s_z, 2 * (NG * l + g))
                for j, (first, n) in enumerate(BANKS):
                    for k in range(n):
                        out_k = PS[0:NP, j, ZC * k:ZC * k + ZC]
                        st = stage[:, first + k, :, :]
                        pe.matmul(out_k[:, 0:66], st[:, 0, :], W[0:CH, C_S:C_S + 66], start=True, stop=True)
                        for m in range(3):
                            o = 66 + V1 * m
                            ins = pe.matmul(out_k[:, o:o + V1], st[0:VF, 1 + m, :], W[0:VF, C_V:C_V + V1],
                                            start=True, stop=True)
                    ins.then_inc(s_conv, 1)

            def transposes(g):
                pe.wait_ge(s_xn, g + 1)
                pe.wait_ge(s_f, NT + GT * g)
                pe.sem_inc(s_go, 1)
                for j, (first, n) in enumerate(BANKS):
                    for k in range(n):
                        for part, (c0, c1) in enumerate(((0, S0), (S0, D))):
                            ins = pe.transpose(PS[0:c1 - c0, TR_BANK[j] + part, NP * k:NP * k + NP],
                                               xn_g[:, first + k, c0:c1], ident[0:NP, 0:NP])
                    ins.then_inc(s_tr, 1)

            def node_group(l, g, last):
                if not last:
                    conv_products(l, g + 1)
                if l == 0:
                    transposes(g)
                    node_products(1, g, xT)

            pe.wait_ge(s_wready, 5)
            for g in range(NG):
                pe.wait_ge(s_xT[g], 32)
                node_products(0, g, x_cols[g])
            pe.wait_ge(s_const, 5)
            pe.wait_ge(s_basef, 1)
            pe.matmul(PS[:, 7, 0:NS], ones_row[:, :], base_f[:, :], start=True, stop=True).then_inc(s_bb, 1)
            pe.wait_ge(s_xtab, 2)
            for l in range(2):
                pe.wait_ge(s_f, NT * (l + 1))
                if l == 1:
                    pe.wait_ge(s_z, 2 * NG)
                    pe.wait_ge(s_wready, 10)
                hidden(l, NS * l, 0, NB * l)
                hidden(l, NS * l + 1, 1, NB * l)
                edge_weights(l, NS * l, 0)
                edge_body(l, 0, False)
                with pe.Fori(1, NB - 1) as b:
                    edge_body(l, b, False)
                edge_body(l, NB - 1, True)
                conv_products(l, 0)
                if l == 0:
                    pe.wait_ge(s_wready, 10)
                with pe.Fori(0, NG - 1) as g:
                    node_group(l, g, False)
                node_group(l, NG - 1, True)


def kernel(x, src, dst, edge_attr_16, edge_attr_4, edge_attr_8, node_vec1, **w):
    import numpy as np
    import concourse.bacc as bacc
    from concourse.bass_utils import run_bass_kernel_spmd

    x, src, dst = np.asarray(x), np.asarray(src), np.asarray(dst)
    x_m = np.concatenate([x[:, :S0], x[:, S0:].reshape(N, V1, 3).transpose(0, 2, 1).reshape(N, VF)], axis=1)
    x_t = x_m.reshape(NP, NT, D).transpose(2, 1, 0).reshape(D, N)
    pad = NS * SE - E

    def by_tile(a):
        return a.reshape(NS * U, P, -1).transpose(1, 0, 2).reshape(P, -1)

    src_t = by_tile(np.pad(src, (0, pad)))
    sh_t = by_tile(np.pad(np.asarray(edge_attr_4), ((0, pad), (0, 0))))
    dst_t = by_tile(np.pad(dst, (0, pad), constant_values=-1))
    dst_rows = np.pad(dst, (0, pad), mode="edge").reshape(NS // 2, 2, SE)

    def radial(a):
        a = np.pad(np.asarray(a), ((0, pad), (0, 16 - a.shape[1])))
        return a.reshape(NS, 2, HC, 16).transpose(0, 1, 3, 2).reshape(NS * 32, HC)

    def weights(fc1, fc2, s_f, s_self, v_f, v_self, alpha, l2s, l2v):
        t = np.zeros((P, C_END), np.float32)
        for k in range(8):
            r = 16 * k
            t[r:r + fc1.shape[0], C_FC1 + 64 * (k % 2):C_FC1 + 64 * (k % 2) + 64] = fc1
        for k in range(2):
            t[64 * k:64 * k + 64, C_FC2:C_FC2 + 192] = fc2
        t[0:S0, C_A:C_A + S0] = s_f
        t[0:S0, C_A + S0:C_A + 2 * S0] = s_self
        for m in range(3):
            r, c = slice(V1 * m, V1 * m + V1), C_B + V1 * m
            t[r, c:c + V1] = v_f
            t[r, c + VF:c + VF + V1] = v_self
        t[VF, C_S] = 1.0
        t[0:VF, C_S + 1:C_S + 2] = alpha
        t[0:VF, C_S + 2:C_S + 66] = l2s
        t[0:VF, C_V:C_V + V1] = l2v
        return t

    w = {k: np.asarray(v) for k, v in w.items()}
    wts0 = weights(w["L0_gnn_Wfc1"], w["L0_gnn_Wfc2"], w["L0_gnn_Wl1_0"], w["L0_gnn_Wsc0"], w["L0_gnn_Wl1_1"],
                   w["L0_gnn_Wsc1"], w["L0_gnn_Wa"], w["L0_gnn_Wl2_s"], w["L0_gnn_Wl2_v"])
    wts1 = weights(w["L1_gnn_fcW1"], w["L1_gnn_fcW2"], w["L1_gnn_W1_s"], w["L1_gnn_W_sc_s"], w["L1_gnn_W1_v"],
                   w["L1_gnn_W_sc_v"], w["L1_gnn_W3"], w["L1_gnn_W2_s"], w["L1_gnn_W2_v"])

    nc = bacc.Bacc("TRN2", target_bir_lowering=False, num_devices=1)
    arrays, args = {}, []
    for name, a in (("x_nodes", x_m), ("x_t", x_t), ("src_t", src_t), ("sh_t", sh_t), ("es0_t", radial(edge_attr_16)),
                    ("es1_t", radial(edge_attr_8)), ("dst_t", dst_t), ("dst_rows", dst_rows),
                    ("attr", np.asarray(node_vec1)), ("wts0", wts0), ("wts1", wts1)):
        a = np.ascontiguousarray(a)
        arrays[name] = a
        args.append(nc.dram_tensor(name, a.shape, mybir.dt.from_np(a.dtype), kind="ExternalInput").ap())
    args.append(nc.dram_tensor("ftab", (N, D), mybir.dt.float32, kind="Internal").ap())
    args.append(nc.dram_tensor("nodes_out", (N, D), mybir.dt.float32, kind="ExternalOutput").ap())
    gnn(nc, *args)
    r = run_bass_kernel_spmd(nc, [arrays], core_ids=[0])
    y = r.results[0]["nodes_out"]
    return np.concatenate([y[:, :S0], y[:, S0:].reshape(N, 3, V1).transpose(0, 2, 1).reshape(N, VF)], axis=1)
```
